# Optimizing a Trainium2 kernel written in Bass

```python
import numpy as np
import jax
import jax.numpy as jnp

def _softmax(x, axis=-1):
    return jax.nn.softmax(x, axis=axis)

def _gelu(x):
    return jax.nn.gelu(x, approximate=True)

def _silu(x):
    return jax.nn.silu(x)

def _sigmoid(x):
    return jax.nn.sigmoid(x)

def _layernorm(x, axis=-1, eps=1e-05):
    m = jnp.mean(x, axis=axis, keepdims=True)
    v = jnp.var(x, axis=axis, keepdims=True)
    return (x - m) / jnp.sqrt(v + eps)

def _scatter_add(tgt, idx, src, axis=0):
    return tgt.at[idx].add(src)

def _segment_sum(src, seg, n):
    return jax.ops.segment_sum(src, seg, n)
kernel_name = 'mk_xattn_ffn_d1_seqx_r2_228e2e'

def setup_inputs(seed: int=0):
    np.random.seed(seed)
    _w = jnp.asarray

    def _rec_inputs():
        import jax
        import jax.numpy as jnp
        _rk = jax.random.key(seed)
        x = -0.000125 + 0.9999 * jax.random.normal(jax.random.fold_in(_rk, 1), (8, 1024, 1024), jnp.float32)
        _lenS = 1024 - jax.random.randint(jax.random.fold_in(_rk, 7), (8,), 0, max(1, 1024 // 4) + 1, jnp.int32)
        _lenS2 = 64 - jax.random.randint(jax.random.fold_in(_rk, 8), (8,), 0, max(1, 64 // 4) + 1, jnp.int32)
        _ctx_2048P = jax.random.normal(jax.random.fold_in(_rk, 11), (8, 16, 1024), jnp.float32)
        _ctx_2048c = jax.random.dirichlet(jax.random.fold_in(_rk, 511), 0.3 * jnp.ones((16,), jnp.float32), (8, 64))
        _ctx_2048t = jnp.einsum('bsk,bkd->bsd', _ctx_2048c, _ctx_2048P)
        _ctx_2048t = _ctx_2048t * jax.lax.rsqrt(jnp.mean(jnp.square(_ctx_2048t)) + 1e-12) * 0.953939
        ctx_2048 = -0.000514642 + 1.00011 * (_ctx_2048t + 0.3 * jax.random.normal(jax.random.fold_in(_rk, 611), (8, 64, 1024), jnp.float32))
        _validS = jnp.arange(1024)[None, :] < _lenS[:, None]
        _validS2 = jnp.arange(64)[None, :] < _lenS2[:, None]
        _causal = jnp.tril(jnp.ones((1024, 1024), dtype=bool))
        mask_BxS2_bk0 = jnp.logical_not(jnp.broadcast_to(_validS2[:, :], (8, 64)))
        return (x, ctx_2048, mask_BxS2_bk0)
    x, ctx_2048, mask_BxS2_bk0 = _rec_inputs()

    def _L0_xattn_setup():
        import jax, jax.numpy as jnp
        import numpy as np
        key = jax.random.key(seed)
        k1, k2, k3 = jax.random.split(key, 3)
        B, S, D, M = (8, 1024, 1024, 128)
        hidden_states = jax.random.normal(k1, (B, S, D), dtype=jnp.float32)
        memory_tokens = jax.random.normal(k2, (B, M, D), dtype=jnp.float32)
        memory_mask = jax.random.randint(k3, (B, M), 0, 2).astype(jnp.bool_)
        return {'hidden_states': hidden_states, 'memory_tokens': memory_tokens, 'memory_mask': memory_mask}
    _L0_xattn_all = _L0_xattn_setup()
    _L0_xattn_in = {k: v for k, v in _L0_xattn_all.items() if k in ()}
    del _L0_xattn_all

    def _L0_ffn_setup():
        import jax, jax.numpy as jnp
        import numpy as np
        NUM_EXPERTS = 8
        RANK = 16
        TOP_K = 2
        SCALING = 32.0 / RANK
        IN_F = 1024
        OUT_F = 1024
        key = jax.random.key(seed)
        k1, k2, k3, k4, k5 = jax.random.split(key, 5)
        B, T = (4, 1024)
        x = jax.random.normal(k1, (B, T, IN_F), dtype=jnp.float32)
        bound_w = 1.0 / np.sqrt(IN_F)
        weight = jax.random.uniform(k2, (OUT_F, IN_F), jnp.float32, -bound_w, bound_w)
        lora_A = jax.random.uniform(k3, (NUM_EXPERTS, RANK, IN_F), jnp.float32, -bound_w, bound_w)
        lora_B = 0.02 * jax.random.normal(k4, (NUM_EXPERTS, OUT_F, RANK), dtype=jnp.float32)
        router_w = jax.random.uniform(k5, (NUM_EXPERTS, IN_F), jnp.float32, -bound_w, bound_w)
        return {'x': x, 'weight': weight, 'lora_A': lora_A, 'lora_B': lora_B, 'router_w': router_w}
    _L0_ffn_all = _L0_ffn_setup()
    _L0_ffn_in = {k: v for k, v in _L0_ffn_all.items() if k in ('weight', 'lora_A', 'lora_B', 'router_w')}
    del _L0_ffn_all
    return {'x': x, 'ctx_2048': ctx_2048, 'mask_BxS2_bk0': mask_BxS2_bk0, 'L0_ffn_weight': _L0_ffn_in['weight'], 'L0_ffn_lora_A': _L0_ffn_in['lora_A'], 'L0_ffn_lora_B': _L0_ffn_in['lora_B'], 'L0_ffn_router_w': _L0_ffn_in['router_w']}

def reference(x, ctx_2048, mask_BxS2_bk0, L0_ffn_weight, L0_ffn_lora_A, L0_ffn_lora_B, L0_ffn_router_w):
    import jax
    import jax.numpy as jnp

    def _L0_xattn_ref(hidden_states, memory_tokens, memory_mask):
        import jax, jax.numpy as jnp
        import numpy as np
        B, S, D = hidden_states.shape
        scale = 1.0 / jnp.sqrt(jnp.asarray(D, hidden_states.dtype))
        scores = jnp.einsum('bsd,bmd->bsm', hidden_states, memory_tokens) * scale
        neg_inf = jnp.asarray(-1e+30, scores.dtype)
        scores = jnp.where(memory_mask[:, None, :], scores, neg_inf)
        attn = jax.nn.softmax(scores, axis=-1)
        readout = jnp.einsum('bsm,bmd->bsd', attn, memory_tokens)
        valid_b = jnp.any(memory_mask, axis=-1)
        out = jnp.where(valid_b[:, None, None], readout, jnp.zeros_like(readout))
        return out

    def _L0_ffn_ref(x, weight, lora_A, lora_B, router_w):
        import jax, jax.numpy as jnp
        import numpy as np
        NUM_EXPERTS = 8
        RANK = 16
        TOP_K = 2
        SCALING = 32.0 / RANK
        IN_F = 1024
        OUT_F = 1024
        B, T, D = x.shape
        N = B * T
        base = jnp.einsum('btd,od->bto', x, weight)
        logits = jnp.einsum('btd,ed->bte', x, router_w)
        probs = jax.nn.softmax(logits, axis=-1)
        topk_vals, topk_idx = jax.lax.top_k(probs, TOP_K)
        topk_vals = topk_vals / topk_vals.sum(axis=-1, keepdims=True)
        w_dense = jnp.zeros((N, NUM_EXPERTS), dtype=x.dtype).at[jnp.arange(N)[:, None], topk_idx.reshape(N, TOP_K)].set(topk_vals.reshape(N, TOP_K))
        x_flat = x.reshape(N, D)
        Ax = jnp.einsum('nd,erd->ner', x_flat, lora_A)
        expert_out = jnp.einsum('ner,ne,eor->no', Ax, w_dense, lora_B) * SCALING
        return base + expert_out.reshape(B, T, OUT_F)
    x = x + _L0_xattn_ref(_layernorm(x, axis=-1), ctx_2048, mask_BxS2_bk0)
    x = x + _L0_ffn_ref(_layernorm(x, axis=-1), L0_ffn_weight, L0_ffn_lora_A, L0_ffn_lora_B, L0_ffn_router_w)
    return x

_drawn_inputs = setup_inputs


def setup_inputs(seed=0):
    import zlib

    import numpy as np

    out = dict(_drawn_inputs(seed))
    spreads = {}
    factors = {}
    for name, (base, spread) in spreads.items():
        noise = np.random.default_rng([zlib.crc32(name.encode()), seed]).standard_normal(out[name].shape)
        drawn = base * np.exp(spread * noise) if base else spread * noise
        out[name] = jnp.asarray(drawn.astype(out[name].dtype))
    for name, factor in factors.items():
        out[name] = (out[name] * factor).astype(out[name].dtype)
    return out
```

```python
import concourse.bass as bass
from concourse import mybir
from contextlib import ExitStack


def xattn_lora_moe_kernel(
    nc: bass.Bass,
    x_in: bass.AP,
    ctx_in: bass.AP,
    ctxT_in: bass.AP,
    mask_in: bass.AP,
    wT_in: bass.AP,
    lrT_in: bass.AP,
    bT_in: bass.AP,
    out: bass.AP,
):
    f32 = mybir.dt.float32
    f32r = mybir.dt.float32r
    u8 = mybir.dt.uint8
    u32 = mybir.dt.uint32
    ALU = mybir.AluOpType
    ACT = mybir.ActivationFunctionType
    AX = mybir.AxisListType

    P = 128
    NT, _, D = x_in.shape
    NB, M, _ = ctx_in.shape
    O = wT_in.shape[2]
    LR = lrT_in.shape[2]
    ER = bT_in.shape[0]
    E = LR - ER
    R = ER // E
    C = D // P
    HC = C // 2
    H = 512
    TPB = NT // NB
    XS = 4
    EPS = 1e-5
    SCALING = 2.0
    SCALE = float(D) ** -0.5
    MASKED = 1e30
    assert D == 2 * H and O == 2 * H and M * 2 == P and ER == P and TPB % XS == 0

    def count(tile, per, more=0):
        b, j = tile
        return b * (TPB * per) + (j * per + more)

    def after(tile, n):
        return (tile[0], tile[1] + n)

    def exists(tile):
        return not isinstance(tile[0], int) or tile[0] * TPB + tile[1] < NT

    def slot(tile):
        return tile[1] % XS

    stack = ExitStack()
    with stack:
        def sb(name, shape, dt=f32):
            return stack.enter_context(nc.sbuf_tensor(name, shape, dt))

        def ps(name, shape):
            return stack.enter_context(nc.psum_tensor(name, shape, f32))

        def sem(name):
            return stack.enter_context(nc.semaphore(name))

        w_hi = sb("w_hi", [P, C, O], f32r)
        w_lo = sb("w_lo", [P, C, O], f32r)
        lr_hi = sb("lr_hi", [P, C, LR], f32r)
        lr_lo = sb("lr_lo", [P, C, LR], f32r)
        b_hi = sb("b_hi", [P, O], f32r)
        b_lo = sb("b_lo", [P, O], f32r)
        w_raw = sb("w_raw", [P, 3, O])
        lr_raw = sb("lr_raw", [P, C, LR])
        b_raw = sb("b_raw", [P, O])
        ctxT = sb("ctxT", [P, C, 2 * M], f32r)
        ctx_hi = sb("ctx_hi", [P, D], f32r)
        ctx_lo = sb("ctx_lo", [P, D], f32r)
        ctxT_raw = sb("ctxT_raw", [P, C, M])
        ctx_raw = sb("ctx_raw", [P, D])
        mask_raw = sb("mask_raw", [P, M], u8)
        mask_f = sb("mask_f", [P, M])
        mask_bias = sb("mask_bias", [P, M])
        any_valid = sb("any_valid", [P, 1])
        x = sb("x", [P, XS, D])
        xn1 = sb("xn1", [P, D])
        xn2 = sb("xn2", [P, D])
        xT1_hi = sb("xT1_hi", [P, C, P], f32r)
        xT1_lo = sb("xT1_lo", [P, C, P], f32r)
        xT2_hi = sb("xT2_hi", [P, 2, C, P], f32r)
        xT2_lo = sb("xT2_lo", [P, 2, C, P], f32r)
        ident = sb("ident", [P, P])
        iota8 = sb("iota8", [P, E])
        neg_half = sb("neg_half", [P, 1])
        stats1 = sb("stats1", [P, 12])
        mean_var1 = sb("mean_var1", [P, 2])
        var_eps1 = sb("var_eps1", [P, 1])
        rstd1 = sb("rstd1", [P, 1])
        stats2 = sb("stats2", [P, 12])
        mean_var2 = sb("mean_var2", [P, 2])
        var_eps2 = sb("var_eps2", [P, 1])
        rstd2 = sb("rstd2", [P, 1])
        s_part = sb("s_part", [P, M])
        s_all = sb("s_all", [P, M])
        neg_max = sb("neg_max", [P, 1])
        e_all = sb("e_all", [P, M])
        e_split = sb("e_split", [P, 2 * M], f32r)
        e_sum = sb("e_sum", [P, 1])
        e_inv = sb("e_inv", [P, 1])
        e_scale = sb("e_scale", [P, 1])
        eT = sb("eT", [P, P], f32r)
        top8 = sb("top8", [P, 8])
        top8_at = sb("top8_at", [P, 8], u32)
        top2_at = sb("top2_at", [P, 2])
        gate_num = sb("gate_num", [P, 2])
        gate_den = sb("gate_den", [P, 1])
        gate_inv = sb("gate_inv", [P, 1])
        gate = sb("gate", [P, 2])
        gate_a = sb("gate_a", [P, E])
        gate_b = sb("gate_b", [P, E])
        w_dense = sb("w_dense", [P, E])
        h = sb("h", [P, ER])
        hT_hi = sb("hT_hi", [P, P], f32r)
        hT_lo = sb("hT_lo", [P, P], f32r)

        base_ps = ps("base_ps", [P, O])
        lr_ps = ps("lr_ps", [P, H])
        s_ps = ps("s_ps", [P, H])
        ro_ps = ps("ro_ps", [P, D])
        tp_ps = ps("tp_ps", [P, D])

        def half(t, i):
            return t[:, i * H:(i + 1) * H]

        def chunks(t, i):
            return t[:, i * HC:(i + 1) * HC, :].rearrange("p c n -> p (c n)")

        x_loaded = [sem(f"x_loaded{s}") for s in range(XS)]
        stored = [sem(f"stored{s}") for s in range(XS)]
        ctx_loaded = [sem(f"ctx_loaded{i}") for i in range(4)]
        w_loaded = [sem(f"w_loaded{c}") for c in range(C)]
        lr_loaded = sem("lr_loaded")
        b_loaded = sem("b_loaded")
        constants_ready = sem("constants_ready")
        ident_zeroed = sem("ident_zeroed")
        waits_alone = sem("waits_alone")
        w_hi_done = sem("w_hi_done")
        w_split = sem("w_split")
        lr_hi_done = sem("lr_hi_done")
        lr_split = sem("lr_split")
        b_hi_done = sem("b_hi_done")
        b_split = sem("b_split")
        ctxT_hi_done = sem("ctxT_hi_done")
        ctxT_split = sem("ctxT_split")
        ctx_hi_done = sem("ctx_hi_done")
        ctx_split = sem("ctx_split")
        mask_step = sem("mask_step")
        ln1_step = sem("ln1_step")
        rstd1_done = sem("rstd1_done")
        xn1_done = sem("xn1_done")
        x1T_done = sem("x1T_done")
        x1T_hi_done = sem("x1T_hi_done")
        x1T_split = sem("x1T_split")
        scores_done = sem("scores_done")
        softmax_step = sem("softmax_step")
        exp_done = sem("exp_done")
        e_split_done = sem("e_split_done")
        eT_done = sem("eT_done")
        eT_copied = sem("eT_copied")
        readout_done = sem("readout_done")
        x1_done = sem("x1_done")
        ln2_step = sem("ln2_step")
        rstd2_done = sem("rstd2_done")
        xn2_done = sem("xn2_done")
        x2T_done = sem("x2T_done")
        x2T_hi_done = sem("x2T_hi_done")
        x2T_split = sem("x2T_split")
        lr_done = sem("lr_done")
        router_step = sem("router_step")
        gate_exp_done = sem("gate_exp_done")
        h_done = sem("h_done")
        hT_done = sem("hT_done")
        hT_hi_done = sem("hT_hi_done")
        hT_split = sem("hT_split")
        base_done = sem("base_done")
        FREE = 2
        out_done = sem("out_done")

        block = stack.enter_context(nc.Block())

        @block.sync
        def _(sp):
            def load_x(tile):
                b, j = tile
                sp.dma_start(x[:, slot(tile), :], x_in[b * TPB + j]).then_inc(x_loaded[slot(tile)], 16)

            def load_ctx(b):
                sp.dma_start(ctxT_raw[:, :, :], ctxT_in[b]).then_inc(ctx_loaded[0], 16)
                sp.dma_start(ctx_raw[0:M, :], ctx_in[b]).then_inc(ctx_loaded[1], 16)
                sp.dma_start(ctx_raw[M:P, :], ctx_in[b]).then_inc(ctx_loaded[2], 16)
                sp.dma_start(mask_raw[:, :], mask_in[b].partition_broadcast(P)).then_inc(ctx_loaded[3], 16)

            load_x((0, 0))
            load_ctx(0)
            sp.dma_start(lr_raw[:, :, :], lrT_in).then_inc(lr_loaded, 16)
            for c in range(C):
                if c >= 3:
                    sp.wait_ge(w_split, c - 2)
                sp.dma_start(w_raw[:, c % 3, :], wT_in[:, c, :]).then_inc(w_loaded[c], 16)
                if c == 2:
                    sp.dma_start(b_raw[:, :], bT_in).then_inc(b_loaded, 16)
                    for j in range(1, XS):
                        load_x((0, j))

            def step(tile):
                b, j = tile
                sp.wait_ge(out_done, count(tile, 2, FREE + 2))
                sp.dma_start(out[b * TPB + j], x[:, slot(tile), :]).then_inc(stored[slot(tile)], 16)
                if exists(after(tile, XS)):
                    sp.wait_ge(stored[slot(tile)], b * (16 * TPB // XS) + 16 * (j // XS + 1))
                    load_x(after(tile, XS))
                if j == 0 and exists((b, TPB)):
                    sp.wait_ge(ctx_split, b + 1)
                    sp.wait_ge(mask_step, b * 3 + 3)
                    load_ctx(b + 1)

            with sp.Fori(0, NB - 1) as b:
                for j in range(TPB):
                    step((b, j))
            for j in range(TPB):
                step((NB - 1, j))
            for s in range(XS):
                sp.wait_ge(stored[s], 16 * NT // XS)

        @block.gpsimd
        def _(pool):
            pool.memset(ident[:, :], 0.0).then_inc(ident_zeroed, 1)
            pool.wait_ge(ident_zeroed, 1)
            pool.affine_select(out=ident[:, :], in_=ident[:, :], compare_op=ALU.not_equal, fill=1.0,
                               base=0, pattern=[[-1, P]], channel_multiplier=1).then_inc(constants_ready, 1)
            for e in range(E):
                pool.memset(iota8[:, e:e + 1], float(e)).then_inc(constants_ready, 1)
            pool.memset(gate_num[:, 0:1], 1.0).then_inc(constants_ready, 1)
            pool.memset(neg_half[:, :], -0.5).then_inc(constants_ready, 1)
            pool.wait_ge(constants_ready, E + 3)

            def rstd(tile, var_eps, out_, steps, done):
                pool.wait_ge(steps, count(tile, 4, 4))
                pool.tensor_tensor(out_[:, :], var_eps[:, :], neg_half[:, :], ALU.pow).then_inc(done, 1)

            def norm1(tile):
                rstd(tile, var_eps1, rstd1, ln1_step, rstd1_done)

            def norm2(tile):
                rstd(tile, var_eps2, rstd2, ln2_step, rstd2_done)

            def step(tile):
                if exists(after(tile, 2)):
                    norm1(after(tile, 2))
                if exists(after(tile, 1)):
                    norm2(after(tile, 1))

            norm1((0, 0))
            norm1((0, 1))
            norm2((0, 0))
            with pool.Fori(0, NB - 1) as b:
                for j in range(TPB):
                    step((b, j))
            for j in range(TPB):
                step((NB - 1, j))

        @block.scalar
        def _(act):
            def ctxT_high(b):
                act.wait_ge(ctx_loaded[0], b * 16 + 16)
                act.wait_ge(scores_done, count((b, 0), 1))
                act.copy(ctxT[:, :, 0:M], ctxT_raw[:, :, :]).then_inc(ctxT_hi_done, 1)

            def ctx_high(b):
                act.wait_ge(ctx_loaded[1], b * 16 + 16)
                act.wait_ge(ctx_loaded[2], b * 16 + 16)
                act.wait_ge(readout_done, count((b, 0), 2))
                act.copy(ctx_hi[:, :], ctx_raw[:, :]).then_inc(ctx_hi_done, 1)

            def x1T_high(tile):
                act.wait_ge(scores_done, count(tile, 1))
                for i in range(2):
                    act.wait_ge(x1T_done, count(tile, 2, i + 1))
                    act.copy(chunks(xT1_hi, i), half(ro_ps, i)).then_inc(x1T_hi_done, 1)

            def softmax_exp(tile):
                act.wait_ge(softmax_step, count(tile, 5, 3))
                act.wait_ge(e_split_done, count(tile, 1))
                act.wait_ge(x1_done, count(tile, 2))
                act.wait_ge(eT_done, count(tile, 1))
                act.activation(e_all[:, :], s_all[:, :], ACT.Exp, bias=neg_max[:, :],
                               accum_out=e_sum[:, :]).then_inc(exp_done, 1)
                act.activation(e_split[:, 0:M], s_all[:, :], ACT.Exp, bias=neg_max[:, :]).then_inc(exp_done, 1)

            def eT_copy(tile):
                act.wait_ge(eT_done, count(tile, 1, 1))
                act.wait_ge(readout_done, count(tile, 2))
                act.copy(eT[:, :], s_ps[:, 0:P]).then_inc(eT_copied, 1)

            def x2T_high(tile):
                for i in range(2):
                    act.wait_ge(x2T_done, count(tile, 2, i + 1))
                    act.copy(chunks(xT2_hi[:, tile[1] % 2], i), half(tp_ps, i)).then_inc(x2T_hi_done, 1)

            def gate_exp(tile):
                act.wait_ge(router_step, count(tile, 9, 1))
                act.activation(gate_num[:, 1:2], top8[:, 0:1], ACT.Exp, bias=top8[:, 1:2],
                               scale=-1.0).then_inc(gate_exp_done, 1)

            def hT_high(tile):
                act.wait_ge(hT_done, count(tile, 1, 1))
                act.copy(hT_hi[:, :], lr_ps[:, 0:P]).then_inc(hT_hi_done, 1)

            def w_high(c):
                act.wait_ge(w_loaded[c], 16)
                act.copy(w_hi[:, c, :], w_raw[:, c % 3, :]).then_inc(w_hi_done, 1)

            def step(tile):
                b, j = tile
                nxt, nxt2 = after(tile, 1), after(tile, 2)
                gate_exp(tile)
                if exists(nxt):
                    softmax_exp(nxt)
                    eT_copy(nxt)
                hT_high(tile)
                if j == TPB - 2 and exists(nxt2):
                    ctxT_high(b + 1)
                    ctx_high(b + 1)
                if exists(nxt2):
                    x1T_high(nxt2)
                if exists(nxt):
                    x2T_high(nxt)

            act.wait_ge(constants_ready, E + 3)
            ctxT_high(0)
            x1T_high((0, 0))
            ctx_high(0)
            act.wait_ge(lr_loaded, 16)
            act.copy(lr_hi[:, :, :], lr_raw[:, :, :]).then_inc(lr_hi_done, 1)
            softmax_exp((0, 0))
            w_high(0)
            eT_copy((0, 0))
            w_high(1)
            w_high(2)
            act.wait_ge(b_loaded, 16)
            act.copy(b_hi[:, :], b_raw[:, :]).then_inc(b_hi_done, 1)
            x1T_high((0, 1))
            w_high(3)
            x2T_high((0, 0))
            for c in range(4, C):
                w_high(c)
            with act.Fori(0, NB - 1) as b:
                for j in range(TPB):
                    step((b, j))
            for j in range(TPB):
                step((NB - 1, j))

        @block.vector
        def _(dve):
            def mask(b):
                dve.wait_ge(ctx_loaded[3], b * 16 + 16)
                dve.tensor_copy(mask_f[:, :], mask_raw[:, :]).then_inc(mask_step, 1)
                dve.wait_ge(mask_step, b * 3 + 1)
                dve.tensor_scalar(mask_bias[:, :], mask_f[:, :], -1.0, MASKED, ALU.add, ALU.mult)\
                   .then_inc(mask_step, 1)
                dve.reduce_max(any_valid[:, :], mask_f[:, :], AX.X).then_inc(mask_step, 1)

            def ctxT_low(b):
                dve.wait_ge(ctxT_hi_done, b + 1)
                dve.tensor_tensor(ctxT[:, :, M:2 * M], ctxT_raw[:, :, :], ctxT[:, :, 0:M].bitcast(f32),
                                  ALU.subtract).then_inc(ctxT_split, 1)

            def ctx_low(b):
                dve.wait_ge(ctx_hi_done, b + 1)
                dve.tensor_tensor(ctx_lo[:, :], ctx_raw[:, :], ctx_hi[:, :].bitcast(f32),
                                  ALU.subtract).then_inc(ctx_split, 1)

            def norm_stats(tile, stats, mean_var, var_eps, steps):
                for i in range(2):
                    dve.bn_stats(stats[:, 6 * i:6 * i + 6], half(x[:, slot(tile), :], i)).then_inc(steps, 1)
                dve.wait_ge(steps, count(tile, 4, 2))
                dve.sem_inc(waits_alone, 1)
                dve.bn_aggr(mean_var[:, :], stats[:, :]).then_inc(steps, 1)
                dve.wait_ge(steps, count(tile, 4, 3))
                dve.tensor_scalar_add(var_eps[:, :], mean_var[:, 1:2], EPS).then_inc(steps, 1)

            def norm1_stats(tile):
                b, j = tile
                dve.wait_ge(x_loaded[slot(tile)], b * (16 * TPB // XS) + 16 * (j // XS + 1))
                norm_stats(tile, stats1, mean_var1, var_eps1, ln1_step)

            def norm1(tile):
                dve.wait_ge(rstd1_done, count(tile, 1, 1))
                dve.wait_ge(x1T_done, count(tile, 2))
                dve.tensor_scalar(xn1[:, :], x[:, slot(tile), :], mean_var1[:, 0:1], rstd1[:, :],
                                  ALU.subtract, ALU.mult).then_inc(xn1_done, 1)

            def x1T_low(tile):
                for i in range(2):
                    dve.wait_ge(x1T_hi_done, count(tile, 2, i + 1))
                    dve.tensor_tensor(chunks(xT1_lo, i), half(ro_ps, i), chunks(xT1_hi, i).bitcast(f32),
                                      ALU.subtract).then_inc(x1T_split, 1)

            def softmax_scores(tile):
                dve.wait_ge(scores_done, count(tile, 1, 1))
                dve.scalar_tensor_tensor(out=s_part[:, :], in0=s_ps[:, M:2 * M], scalar=SCALE,
                                         in1=mask_bias[:, :], op0=ALU.mult, op1=ALU.add).then_inc(softmax_step, 1)
                dve.wait_ge(softmax_step, count(tile, 5, 1))
                dve.scalar_tensor_tensor(out=s_all[:, :], in0=s_ps[:, 0:M], scalar=SCALE,
                                         in1=s_part[:, :], op0=ALU.mult, op1=ALU.add).then_inc(softmax_step, 1)
                dve.wait_ge(softmax_step, count(tile, 5, 2))
                dve.tensor_reduce(out=neg_max[:, :], in_=s_all[:, :], axis=AX.X, op=ALU.max,
                                  negate=True).then_inc(softmax_step, 1)

            def softmax_split(tile):
                dve.wait_ge(exp_done, count(tile, 2, 2))
                dve.tensor_tensor(e_split[:, M:2 * M], e_all[:, :], e_split[:, 0:M].bitcast(f32),
                                  ALU.subtract).then_inc(e_split_done, 1)
                dve.reciprocal(e_inv[:, :], e_sum[:, :]).then_inc(softmax_step, 1)
                dve.wait_ge(softmax_step, count(tile, 5, 4))
                dve.tensor_tensor(e_scale[:, :], e_inv[:, :], any_valid[:, :], ALU.mult).then_inc(softmax_step, 1)

            def add_readout(tile):
                dve.wait_ge(softmax_step, count(tile, 5, 5))
                for i in range(2):
                    xh = half(x[:, slot(tile), :], i)
                    dve.wait_ge(readout_done, count(tile, 2, i + 1))
                    dve.scalar_tensor_tensor(out=xh, in0=half(ro_ps, i), scalar=e_scale[:, :], in1=xh,
                                             op0=ALU.mult, op1=ALU.add).then_inc(x1_done, 1)

            def norm2_stats(tile):
                dve.wait_ge(x1_done, count(tile, 2, 2))
                norm_stats(tile, stats2, mean_var2, var_eps2, ln2_step)

            def norm2(tile):
                dve.wait_ge(rstd2_done, count(tile, 1, 1))
                dve.wait_ge(x2T_done, count(tile, 2))
                dve.tensor_scalar(xn2[:, :], x[:, slot(tile), :], mean_var2[:, 0:1], rstd2[:, :],
                                  ALU.subtract, ALU.mult).then_inc(xn2_done, 1)

            def x2T_low(tile):
                k = tile[1] % 2
                for i in range(2):
                    dve.wait_ge(x2T_hi_done, count(tile, 2, i + 1))
                    dve.tensor_tensor(chunks(xT2_lo[:, k], i), half(tp_ps, i), chunks(xT2_hi[:, k], i).bitcast(f32),
                                      ALU.subtract).then_inc(x2T_split, 1)

            def router_top(tile):
                logits = lr_ps[:, ER:ER + E]
                dve.wait_ge(lr_done, count(tile, 1, 1))
                dve.sem_inc(waits_alone, 1)
                dve.max(top8[:, :], logits).then_inc(router_step, 1)
                dve.wait_ge(router_step, count(tile, 9, 1))
                dve.sem_inc(waits_alone, 1)
                dve.max_index(top8_at[:, :], top8[:, :], logits).then_inc(router_step, 1)
                dve.wait_ge(router_step, count(tile, 9, 2))
                dve.tensor_copy(top2_at[:, :], top8_at[:, 0:2]).then_inc(router_step, 1)

            def router_gate(tile):
                dve.wait_ge(gate_exp_done, count(tile, 1, 1))
                dve.tensor_scalar_add(gate_den[:, :], gate_num[:, 1:2], 1.0).then_inc(router_step, 1)
                dve.wait_ge(router_step, count(tile, 9, 4))
                dve.reciprocal(gate_inv[:, :], gate_den[:, :]).then_inc(router_step, 1)
                dve.wait_ge(router_step, count(tile, 9, 5))
                dve.tensor_scalar(gate[:, :], gate_num[:, :], gate_inv[:, :], SCALING, ALU.mult, ALU.mult)\
                   .then_inc(router_step, 1)
                dve.wait_ge(router_step, count(tile, 9, 6))
                dve.tensor_scalar(gate_a[:, :], iota8[:, :], top2_at[:, 0:1], gate[:, 0:1], ALU.is_equal, ALU.mult)\
                   .then_inc(router_step, 1)
                dve.tensor_scalar(gate_b[:, :], iota8[:, :], top2_at[:, 1:2], gate[:, 1:2], ALU.is_equal, ALU.mult)\
                   .then_inc(router_step, 1)
                dve.wait_ge(router_step, count(tile, 9, 8))
                dve.tensor_tensor(w_dense[:, :], gate_a[:, :], gate_b[:, :], ALU.add).then_inc(router_step, 1)
                dve.wait_ge(router_step, count(tile, 9, 9))
                dve.tensor_tensor(h[:, :].rearrange("p (e r) -> p e r", r=R),
                                  lr_ps[:, 0:ER].rearrange("p (e r) -> p e r", r=R),
                                  w_dense[:, :].unsqueeze(2).to_broadcast([P, E, R]),
                                  ALU.mult).then_inc(h_done, 1)

            def hT_low(tile):
                dve.wait_ge(hT_hi_done, count(tile, 1, 1))
                dve.tensor_tensor(hT_lo[:, :], lr_ps[:, 0:P], hT_hi[:, :].bitcast(f32),
                                  ALU.subtract).then_inc(hT_split, 1)

            def add_base(tile):
                for i in range(2):
                    xh = half(x[:, slot(tile), :], i)
                    dve.wait_ge(base_done, count(tile, 2, i + 1))
                    dve.tensor_tensor(xh, half(base_ps, i), xh, ALU.add).then_inc(out_done, 1)

            def w_low(c):
                dve.wait_ge(w_hi_done, c + 1)
                dve.tensor_tensor(w_lo[:, c, :], w_raw[:, c % 3, :], w_hi[:, c, :].bitcast(f32),
                                  ALU.subtract).then_inc(w_split, 1)

            def step(tile):
                b, j = tile
                nxt, nxt2 = after(tile, 1), after(tile, 2)
                router_top(tile)
                if exists(nxt):
                    softmax_scores(nxt)
                router_gate(tile)
                if exists(nxt):
                    softmax_split(nxt)
                if exists(nxt2):
                    norm1_stats(nxt2)
                    norm1(nxt2)
                if exists(nxt):
                    add_readout(nxt)
                    norm2_stats(nxt)
                hT_low(tile)
                if exists(nxt):
                    norm2(nxt)
                if exists(nxt2):
                    x1T_low(nxt2)
                if exists(nxt):
                    x2T_low(nxt)
                if j == TPB - 2 and exists(nxt2):
                    ctxT_low(b + 1)
                    ctx_low(b + 1)
                    mask(b + 1)
                add_base(tile)

            dve.sem_inc(out_done, FREE)
            dve.wait_ge(constants_ready, E + 3)
            norm1_stats((0, 0))
            norm1((0, 0))
            ctxT_low(0)
            mask(0)
            x1T_low((0, 0))
            ctx_low(0)
            dve.wait_ge(mask_step, 3)
            softmax_scores((0, 0))
            dve.wait_ge(lr_hi_done, 1)
            dve.tensor_tensor(lr_lo[:, :, :], lr_raw[:, :, :], lr_hi[:, :, :].bitcast(f32),
                              ALU.subtract).then_inc(lr_split, 1)
            softmax_split((0, 0))
            w_low(0)
            w_low(1)
            add_readout((0, 0))
            norm2_stats((0, 0))
            norm1_stats((0, 1))
            norm2((0, 0))
            norm1((0, 1))
            w_low(2)
            dve.wait_ge(b_hi_done, 1)
            dve.tensor_tensor(b_lo[:, :], b_raw[:, :], b_hi[:, :].bitcast(f32), ALU.subtract).then_inc(b_split, 1)
            x1T_low((0, 1))
            w_low(3)
            x2T_low((0, 0))
            for c in range(4, C):
                w_low(c)
            with dve.Fori(0, NB - 1) as b:
                for j in range(TPB):
                    step((b, j))
            for j in range(TPB):
                step((NB - 1, j))

        @block.tensor
        def _(pe):
            def three(out_, a_hi, a_lo, w_h, w_l, start, stop):
                pe.matmul(out_, a_hi, w_h, start=start, stop=False)
                pe.matmul(out_, a_hi, w_l, start=False, stop=False)
                return pe.matmul(out_, a_lo, w_h, start=False, stop=stop)

            def transposes(ps_, src, done):
                for c in range(C):
                    mm = pe.transpose(ps_[:, c * P:(c + 1) * P], src[:, c * P:(c + 1) * P], ident[:, :])
                    if c % HC == HC - 1:
                        mm.then_inc(done, 1)

            def x1_transposes(tile):
                pe.wait_ge(xn1_done, count(tile, 1, 1))
                pe.wait_ge(x1_done, count(tile, 2))
                transposes(ro_ps, xn1, x1T_done)

            def scores(tile):
                b, j = tile
                if j % TPB == 0:
                    pe.wait_ge(ctxT_split, b + j // TPB + 1)
                pe.wait_ge(x1T_split, count(tile, 2, 2))
                pe.wait_ge(eT_copied, count(tile, 1))
                for c in range(C):
                    pe.matmul(s_ps[:, 0:2 * M], xT1_hi[:, c, :], ctxT[:, c, :], start=(c == 0), stop=False)
                    mm = pe.matmul(s_ps[:, 0:2 * M], xT1_lo[:, c, :], ctxT[:, c, :], start=False, stop=(c == C - 1))
                mm.then_inc(scores_done, 1)

            def e_transpose(tile):
                pe.wait_ge(e_split_done, count(tile, 1, 1))
                pe.transpose(s_ps[:, 0:P], e_split[:, :].bitcast(f32), ident[:, :]).then_inc(eT_done, 1)

            def readout(tile):
                b, j = tile
                if j % TPB == 0:
                    pe.wait_ge(ctx_split, b + j // TPB + 1)
                pe.wait_ge(eT_copied, count(tile, 1, 1))
                for i in range(2):
                    pe.matmul(half(ro_ps, i), eT[:, :], half(ctx_hi, i), start=True, stop=False)
                    pe.matmul(half(ro_ps, i), eT[:, :], half(ctx_lo, i), start=False, stop=True)\
                      .then_inc(readout_done, 1)

            def x2_transposes(tile):
                pe.wait_ge(xn2_done, count(tile, 1, 1))
                pe.wait_ge(x2T_split, count(tile, 2))
                transposes(tp_ps, xn2, x2T_done)

            def lora_first(tile):
                k = tile[1] % 2
                if tile[1] == 0:
                    pe.wait_ge(lr_split, 1)
                pe.wait_ge(x2T_split, count(tile, 2, 2))
                for c in range(C):
                    mm = three(lr_ps[:, 0:LR], xT2_hi[:, k, c, :], xT2_lo[:, k, c, :],
                               lr_hi[:, c, :], lr_lo[:, c, :], c == 0, c == C - 1)
                mm.then_inc(lr_done, 1)

            def base(tile, c):
                k = tile[1] % 2
                if tile[1] == 0:
                    pe.wait_ge(w_split, c + 1)
                if c == 0:
                    pe.wait_ge(out_done, count(tile, 2, FREE))
                for a, w in ((xT2_hi, w_hi), (xT2_hi, w_lo), (xT2_lo, w_hi)):
                    for i in range(2):
                        pe.matmul(half(base_ps, i), a[:, k, c, :], half(w[:, c, :], i),
                                  start=(c == 0 and a is xT2_hi and w is w_hi), stop=False)

            def h_transpose(tile):
                pe.wait_ge(h_done, count(tile, 1, 1))
                pe.transpose(lr_ps[:, 0:P], h[:, :], ident[:, :]).then_inc(hT_done, 1)

            def lora_second(tile):
                if tile[1] == 0:
                    pe.wait_ge(b_split, 1)
                pe.wait_ge(hT_split, count(tile, 1, 1))
                for i in range(2):
                    three(half(base_ps, i), hT_hi[:, :], hT_lo[:, :], half(b_hi, i), half(b_lo, i), False, True)\
                        .then_inc(base_done, 1)

            def step(tile):
                nxt, nxt2 = after(tile, 1), after(tile, 2)
                lora_first(tile)
                if exists(nxt):
                    scores(nxt)
                base(tile, 0)
                base(tile, 1)
                if exists(nxt):
                    e_transpose(nxt)
                base(tile, 2)
                if exists(nxt):
                    readout(nxt)
                h_transpose(tile)
                base(tile, 3)
                base(tile, 4)
                base(tile, 5)
                if exists(nxt2):
                    x1_transposes(nxt2)
                base(tile, 6)
                if exists(nxt):
                    x2_transposes(nxt)
                base(tile, 7)
                lora_second(tile)

            pe.wait_ge(constants_ready, E + 3)
            x1_transposes((0, 0))
            scores((0, 0))
            e_transpose((0, 0))
            readout((0, 0))
            x1_transposes((0, 1))
            x2_transposes((0, 0))
            with pe.Fori(0, NB - 1) as b:
                for j in range(TPB):
                    step((b, j))
            for j in range(TPB):
                step((NB - 1, j))


def kernel(x, ctx_2048, mask_BxS2_bk0, L0_ffn_weight, L0_ffn_lora_A, L0_ffn_lora_B, L0_ffn_router_w):
    import numpy as np
    import concourse.bacc as bacc
    from concourse import mybir as mb
    from concourse.bass_utils import run_bass_kernel_spmd

    P = 128

    def by_contraction(a):
        n, d = a.shape
        return np.ascontiguousarray(a.T.reshape(d // P, P, n).transpose(1, 0, 2))

    x, ctx, mask = np.asarray(x), np.asarray(ctx_2048), np.asarray(mask_BxS2_bk0)
    weight, lora_a, lora_b, router = (
        np.asarray(a) for a in (L0_ffn_weight, L0_ffn_lora_A, L0_ffn_lora_B, L0_ffn_router_w))
    B, S, D = x.shape
    E, R, _ = lora_a.shape
    O = weight.shape[0]
    arrays = {
        "x": np.ascontiguousarray(x.reshape(B * S // P, P, D)),
        "ctx": np.ascontiguousarray(ctx),
        "ctxT": np.stack([by_contraction(c) for c in ctx]),
        "mask": np.ascontiguousarray(mask),
        "wT": by_contraction(weight),
        "lrT": by_contraction(np.concatenate([lora_a.reshape(E * R, D), router], axis=0)),
        "bT": np.ascontiguousarray(lora_b.transpose(0, 2, 1).reshape(E * R, O)),
    }
    nc = bacc.Bacc("TRN2", target_bir_lowering=False, num_devices=1)
    args = [nc.dram_tensor(f"in_{n}", a.shape, mb.dt.from_np(a.dtype), kind="ExternalInput").ap()
            for n, a in arrays.items()]
    out = nc.dram_tensor("out", (B * S // P, P, O), mb.dt.float32, kind="ExternalOutput").ap()
    xattn_lora_moe_kernel(nc, *args, out)
    r = run_bass_kernel_spmd(nc, [{f"in_{n}": a for n, a in arrays.items()}], core_ids=[0])
    return r.results[0]["out"].reshape(B, S, O)
```

```python
import concourse.bass as bass
from concourse import mybir
from contextlib import ExitStack


def xattn_lora_moe_kernel(
    nc: bass.Bass,
    x_in: bass.AP,
    xT_in: bass.AP,
    ctx_in: bass.AP,
    mask_in: bass.AP,
    wT_in: bass.AP,
    bT_in: bass.AP,
    out: bass.AP,
):
    f32 = mybir.dt.float32
    f32r = mybir.dt.float32r
    u8 = mybir.dt.uint8
    u32 = mybir.dt.uint32
    ALU = mybir.AluOpType
    ACT = mybir.ActivationFunctionType
    AX = mybir.AxisListType

    P = 128
    NT, _, D = x_in.shape
    NB, M, _ = ctx_in.shape
    ER, O = bT_in.shape
    WC = wT_in.shape[2]
    LR = WC - O
    E = LR - ER
    R = ER // E
    C = D // P
    HC = C // 2
    H = 512
    TPB = NT // NB
    T2 = 2 * P
    XS = 4
    EPS = 1e-5
    SCALING = 2.0
    SCALE = float(D) ** -0.5
    MASKED = 1e30
    assert D == 2 * H and O == 2 * H and M * 2 == P and ER == P and TPB % XS == 0
    SIDE = WC // 6 * 2
    W0 = O - 2 * SIDE
    GROUPS = [(0, W0 + LR), (W0 + LR, SIDE), (W0 + LR + SIDE, SIDE)]
    OUTS = [(0, W0), (W0, SIDE), (W0 + SIDE, SIDE)]
    G = len(GROUPS)
    WPARTS = 4
    CP = C // WPARTS

    def count(tile, per, more=0):
        b, j = tile
        return b * (TPB * per) + (j * per + more)

    def after(tile, n):
        return (tile[0], tile[1] + n)

    def exists(tile):
        return not isinstance(tile[0], int) or tile[0] * TPB + tile[1] < NT

    def slot(tile):
        return tile[1] % XS

    def pairs(tile, per, more=0):
        b, j = tile
        return b * (TPB // 2 * per) + (j // 2 * per + more)

    stack = ExitStack()
    with stack:
        def sb(name, shape, dt=f32):
            return stack.enter_context(nc.sbuf_tensor(name, shape, dt))

        def ps(name, shape):
            return stack.enter_context(nc.psum_tensor(name, shape, f32))

        def sem(name):
            return stack.enter_context(nc.semaphore(name))

        w_hi = sb("w_hi", [P, C, WC], f32r)
        w_lo = sb("w_lo", [P, C, WC], f32r)
        b_hi = sb("b_hi", [P, O], f32r)
        b_lo = sb("b_lo", [P, O], f32r)
        w_raw = [sb(f"w_raw{i}", [P, C, GROUPS[0][1]]) for i in range(2)]
        b_raw = sb("b_raw", [P, O])
        ctxT = sb("ctxT", [P, C, 2 * M], f32r)
        ctx_hi = sb("ctx_hi", [P, D], f32r)
        ctx_lo = sb("ctx_lo", [P, D], f32r)
        ctx_raw = sb("ctx_raw", [P, D])
        ctx_centred = sb("ctx_centred", [P, D])
        ctx_stats = sb("ctx_stats", [P, 12])
        ctx_mean_var = sb("ctx_mean_var", [P, 2])
        mask_raw = sb("mask_raw", [P, M], u8)
        mask_f = sb("mask_f", [P, M])
        mask_bias = sb("mask_bias", [P, M])
        any_valid = sb("any_valid", [P, 1])
        x = sb("x", [P, XS, D])
        xn2 = sb("xn2", [P, D])
        xT_raw = sb("xT_raw", [P, 2, C, T2])
        xT_hi = sb("xT_hi", [P, C, T2], f32r)
        xT_lo = sb("xT_lo", [P, C, T2], f32r)
        sT = sb("sT", [P, T2])
        xT2_hi = sb("xT2_hi", [P, 2, C, P], f32r)
        xT2_lo = sb("xT2_lo", [P, 2, C, P], f32r)
        ident = sb("ident", [P, P])
        iota8 = sb("iota8", [P, E])
        neg_half = sb("neg_half", [P, 1])
        stats1 = sb("stats1", [P, 12])
        mean_var1 = sb("mean_var1", [P, 2])
        var_eps1 = sb("var_eps1", [P, 1])
        rstd1 = sb("rstd1", [P, 1])
        stats2 = sb("stats2", [P, 12])
        mean_var2 = sb("mean_var2", [P, 2])
        var_eps2 = sb("var_eps2", [P, 1])
        rstd2 = sb("rstd2", [P, 1])
        s_part = sb("s_part", [P, M])
        s_all = sb("s_all", [P, M])
        neg_max = sb("neg_max", [P, 1])
        e_all = sb("e_all", [P, M])
        e_split = sb("e_split", [P, 2 * M], f32r)
        e_sum = sb("e_sum", [P, 1])
        e_inv = sb("e_inv", [P, 1])
        e_scale = sb("e_scale", [P, 1])
        eT = sb("eT", [P, P], f32r)
        top8 = sb("top8", [P, 8])
        top8_at = sb("top8_at", [P, 8], u32)
        top2_at = sb("top2_at", [P, 2])
        gate_num = sb("gate_num", [P, 2])
        gate_den = sb("gate_den", [P, 1])
        gate_inv = sb("gate_inv", [P, 1])
        gate = sb("gate", [P, 2])
        gate_a = sb("gate_a", [P, E])
        gate_b = sb("gate_b", [P, E])
        w_dense = sb("w_dense", [P, E])
        h = sb("h", [P, ER])
        hT_hi = sb("hT_hi", [P, P], f32r)
        hT_lo = sb("hT_lo", [P, P], f32r)

        base_ps = [ps(f"base_ps{g}", [P, H]) for g in range(G)]
        s_ps = ps("s_ps", [P, H])
        ro_ps = ps("ro_ps", [P, D])
        tp_ps = ps("tp_ps", [P, D])
        st_ps = ro_ps[:, 0:2 * M]
        et_ps = ro_ps[:, H:H + P]
        lr_ps = base_ps[0][:, W0:W0 + LR]

        def half(t, i):
            return t[:, i * H:(i + 1) * H]

        def chunks(t, i):
            return t[:, i * HC:(i + 1) * HC, :].rearrange("p c n -> p (c n)")

        def both_rows(t, i):
            return half(t, i).rearrange("p (c k m) -> p c k m", c=HC, k=2)[:, :, 0, :]

        def c_half(t, i):
            return t[:, i * HC:(i + 1) * HC, :]

        def w_columns(t, g):
            c0, n = GROUPS[g]
            return t[:, :, c0:c0 + n]

        def w_part(t, g, r):
            return w_columns(t, g)[:, r * CP:(r + 1) * CP, :]

        def raw_part(g, r):
            return w_raw[g % 2][:, r * CP:(r + 1) * CP, 0:GROUPS[g][1]]

        x_loaded = [sem(f"x_loaded{s}") for s in range(XS)]
        stored = [sem(f"stored{s}") for s in range(XS)]
        xT_loaded = [sem(f"xT_loaded{i}") for i in range(2)]
        ctx_loaded = [sem(f"ctx_loaded{i}") for i in range(3)]
        w_loaded = [sem(f"w_loaded{g}") for g in range(G)]
        b_loaded = sem("b_loaded")
        constants_ready = sem("constants_ready")
        ident_zeroed = sem("ident_zeroed")
        waits_alone = sem("waits_alone")
        w_hi_done = [sem(f"w_hi_done{g}") for g in range(G)]
        w_split = [sem(f"w_split{g}") for g in range(G)]
        b_hi_done = sem("b_hi_done")
        b_split = sem("b_split")
        ctx_step = sem("ctx_step")
        ctxT_done = sem("ctxT_done")
        ctxT_hi_done = sem("ctxT_hi_done")
        ctxT_split = sem("ctxT_split")
        ctx_hi_done = sem("ctx_hi_done")
        ctx_split = sem("ctx_split")
        mask_step = sem("mask_step")
        ln1_step = sem("ln1_step")
        rstd1_done = sem("rstd1_done")
        xT_hi_done = sem("xT_hi_done")
        xT_split = sem("xT_split")
        sT_done = sem("sT_done")
        sT_copied = sem("sT_copied")
        scores_done = sem("scores_done")
        softmax_step = sem("softmax_step")
        exp_done = sem("exp_done")
        e_split_done = sem("e_split_done")
        eT_done = sem("eT_done")
        eT_copied = sem("eT_copied")
        readout_done = sem("readout_done")
        x1_done = sem("x1_done")
        ln2_step = sem("ln2_step")
        rstd2_done = sem("rstd2_done")
        xn2_done = sem("xn2_done")
        x2T_done = sem("x2T_done")
        x2T_hi_done = sem("x2T_hi_done")
        x2T_split = sem("x2T_split")
        lr_done = sem("lr_done")
        router_step = sem("router_step")
        gate_exp_done = sem("gate_exp_done")
        h_done = sem("h_done")
        hT_done = sem("hT_done")
        hT_hi_done = sem("hT_hi_done")
        hT_split = sem("hT_split")
        base_done = sem("base_done")
        FREE = G
        out_done = sem("out_done")

        block = stack.enter_context(nc.Block())

        def w_low(engine, g, r):
            engine.wait_ge(w_hi_done[g], r + 1)
            engine.tensor_tensor(w_part(w_lo, g, r), raw_part(g, r), w_part(w_hi, g, r).bitcast(f32),
                                 ALU.subtract).then_inc(w_split[g], 1)

        @block.sync
        def _(sp):
            def load_x(tile):
                b, j = tile
                sp.dma_start(x[:, slot(tile), :], x_in[b * TPB + j]).then_inc(x_loaded[slot(tile)], 16)

            def load_xT(tile):
                b, j = tile
                k = j // 2 % 2
                sp.dma_start(xT_raw[:, k], xT_in[b * (TPB // 2) + j // 2]).then_inc(xT_loaded[k], 16)

            def load_ctx(b):
                sp.dma_start(ctx_raw[0:M, :], ctx_in[b]).then_inc(ctx_loaded[0], 16)
                sp.dma_start(ctx_raw[M:P, :], ctx_in[b]).then_inc(ctx_loaded[1], 16)
                sp.dma_start(mask_raw[:, :], mask_in[b].partition_broadcast(P)).then_inc(ctx_loaded[2], 16)

            def load_w(g):
                c0, n = GROUPS[g]
                sp.dma_start(w_raw[g % 2][:, :, 0:n], wT_in[:, :, c0:c0 + n]).then_inc(w_loaded[g], 16)

            load_ctx(0)
            load_xT((0, 0))
            load_x((0, 0))
            load_w(0)
            load_w(1)
            load_x((0, 1))
            load_xT((0, 2))
            sp.wait_ge(w_split[0], WPARTS)
            load_w(2)
            load_x((0, 2))
            sp.dma_start(b_raw[:, :], bT_in).then_inc(b_loaded, 16)
            load_x((0, 3))

            def step(tile):
                b, j = tile
                if j % 2 == 0 and exists(after(tile, 4)):
                    sp.wait_ge(xT_split, pairs(tile, 2, 2))
                    load_xT(after(tile, 4))
                sp.wait_ge(out_done, count(tile, G, FREE + G))
                sp.dma_start(out[b * TPB + j], x[:, slot(tile), :]).then_inc(stored[slot(tile)], 16)
                if exists(after(tile, XS)):
                    sp.wait_ge(stored[slot(tile)], b * (16 * TPB // XS) + 16 * (j // XS + 1))
                    load_x(after(tile, XS))
                if j == 0 and exists((b, TPB)):
                    sp.wait_ge(ctx_split, b + 1)
                    sp.wait_ge(mask_step, b * 3 + 3)
                    load_ctx(b + 1)

            with sp.Fori(0, NB - 1) as b:
                for j in range(TPB):
                    step((b, j))
            for j in range(TPB):
                step((NB - 1, j))
            for s in range(XS):
                sp.wait_ge(stored[s], 16 * NT // XS)

        @block.gpsimd
        def _(pool):
            pool.memset(ident[:, :], 0.0).then_inc(ident_zeroed, 1)
            pool.wait_ge(ident_zeroed, 1)
            pool.affine_select(out=ident[:, :], in_=ident[:, :], compare_op=ALU.not_equal, fill=1.0,
                               base=0, pattern=[[-1, P]], channel_multiplier=1).then_inc(constants_ready, 1)
            for e in range(E):
                pool.memset(iota8[:, e:e + 1], float(e)).then_inc(constants_ready, 1)
            pool.memset(gate_num[:, 0:1], 1.0).then_inc(constants_ready, 1)
            pool.memset(neg_half[:, :], -0.5).then_inc(constants_ready, 1)
            pool.wait_ge(constants_ready, E + 3)

            def rstd(tile, var_eps, out_, steps, done):
                pool.wait_ge(steps, count(tile, 4, 4))
                pool.tensor_tensor(out_[:, :], var_eps[:, :], neg_half[:, :], ALU.pow).then_inc(done, 1)

            def norm1(tile):
                rstd(tile, var_eps1, rstd1, ln1_step, rstd1_done)

            def norm2(tile):
                rstd(tile, var_eps2, rstd2, ln2_step, rstd2_done)

            def step(tile):
                if exists(after(tile, 2)):
                    norm1(after(tile, 2))
                if exists(after(tile, 1)):
                    norm2(after(tile, 1))

            norm1((0, 0))
            norm2((0, 0))
            norm1((0, 1))
            for r in range(WPARTS):
                w_low(pool, G - 1, r)
            with pool.Fori(0, NB - 1) as b:
                for j in range(TPB):
                    step((b, j))
            for j in range(TPB):
                step((NB - 1, j))

        @block.scalar
        def _(act):
            def ctxT_high(b):
                for i in range(2):
                    act.wait_ge(ctxT_done, b * 2 + i + 1)
                    act.copy(ctxT[:, i * HC:(i + 1) * HC, 0:M], both_rows(tp_ps, i)).then_inc(ctxT_hi_done, 1)

            def ctx_high(b):
                act.wait_ge(ctx_loaded[0], b * 16 + 16)
                act.wait_ge(ctx_loaded[1], b * 16 + 16)
                act.wait_ge(readout_done, count((b, 0), 2))
                act.copy(ctx_hi[:, :], ctx_raw[:, :]).then_inc(ctx_hi_done, 1)

            def xT_high(tile, i):
                b, j = tile
                k = j // 2 % 2
                act.wait_ge(xT_loaded[k], b * (16 * TPB // 4) + 16 * (j // 4 + 1))
                act.wait_ge(sT_done, pairs(tile, 1))
                act.copy(c_half(xT_hi, i), c_half(xT_raw[:, k], i)).then_inc(xT_hi_done, 1)

            def sT_copy(tile):
                act.wait_ge(sT_done, pairs(tile, 1, 1))
                act.wait_ge(scores_done, count(tile, 1))
                act.copy(sT[:, :], s_ps[:, 0:T2]).then_inc(sT_copied, 1)

            def softmax_exp(tile):
                act.wait_ge(softmax_step, count(tile, 5, 3))
                act.wait_ge(e_split_done, count(tile, 1))
                act.wait_ge(x1_done, count(tile, 2))
                act.wait_ge(eT_done, count(tile, 1))
                act.activation(e_all[:, :], s_all[:, :], ACT.Exp, bias=neg_max[:, :],
                               accum_out=e_sum[:, :]).then_inc(exp_done, 1)
                act.activation(e_split[:, 0:M], s_all[:, :], ACT.Exp, bias=neg_max[:, :]).then_inc(exp_done, 1)

            def eT_copy(tile):
                act.wait_ge(eT_done, count(tile, 1, 1))
                act.wait_ge(readout_done, count(tile, 2))
                act.copy(eT[:, :], et_ps).then_inc(eT_copied, 1)

            def x2T_high(tile):
                for i in range(2):
                    act.wait_ge(x2T_done, count(tile, 2, i + 1))
                    act.copy(chunks(xT2_hi[:, tile[1] % 2], i), half(tp_ps, i)).then_inc(x2T_hi_done, 1)

            def gate_exp(tile):
                act.wait_ge(router_step, count(tile, 9, 1))
                act.activation(gate_num[:, 1:2], top8[:, 0:1], ACT.Exp, bias=top8[:, 1:2],
                               scale=-1.0).then_inc(gate_exp_done, 1)

            def hT_high(tile):
                act.wait_ge(hT_done, count(tile, 1, 1))
                act.copy(hT_hi[:, :], s_ps[:, 0:P]).then_inc(hT_hi_done, 1)

            def w_high(g, r):
                act.wait_ge(w_loaded[g], 16)
                act.copy(w_part(w_hi, g, r), raw_part(g, r)).then_inc(w_hi_done[g], 1)

            def step(tile):
                b, j = tile
                nxt, nxt2 = after(tile, 1), after(tile, 2)
                if exists(nxt):
                    softmax_exp(nxt)
                if exists(after(tile, 2 + j % 2)):
                    xT_high(after(tile, 2 + j % 2), 1 - j % 2)
                if exists(nxt):
                    eT_copy(nxt)
                gate_exp(tile)
                if j == TPB - 3 and exists((b, TPB)):
                    ctxT_high(b + 1)
                hT_high(tile)
                if exists(nxt):
                    x2T_high(nxt)
                if j == TPB - 2 and exists((b, TPB)):
                    ctx_high(b + 1)
                if j % 2 == 0 and exists(nxt2):
                    sT_copy(nxt2)

            act.wait_ge(constants_ready, E + 3)
            ctx_high(0)
            xT_high((0, 0), 0)
            ctxT_high(0)
            xT_high((0, 0), 1)
            w_high(0, 0)
            w_high(0, 1)
            sT_copy((0, 0))
            w_high(0, 2)
            softmax_exp((0, 0))
            w_high(0, 3)
            eT_copy((0, 0))
            for r in range(WPARTS):
                w_high(1, r)
            x2T_high((0, 0))
            xT_high((0, 2), 0)
            for r in range(WPARTS):
                w_high(2, r)
            act.wait_ge(b_loaded, 16)
            act.copy(b_hi[:, :], b_raw[:, :]).then_inc(b_hi_done, 1)
            with act.Fori(0, NB - 1) as b:
                for j in range(TPB):
                    step((b, j))
            for j in range(TPB):
                step((NB - 1, j))

        @block.vector
        def _(dve):
            def mask(b):
                dve.wait_ge(ctx_loaded[2], b * 16 + 16)
                dve.tensor_copy(mask_f[:, :], mask_raw[:, :]).then_inc(mask_step, 1)
                dve.wait_ge(mask_step, b * 3 + 1)
                dve.tensor_scalar(mask_bias[:, :], mask_f[:, :], -1.0, MASKED, ALU.add, ALU.mult)\
                   .then_inc(mask_step, 1)
                dve.reduce_max(any_valid[:, :], mask_f[:, :], AX.X).then_inc(mask_step, 1)

            def ctx_centre(b):
                dve.wait_ge(ctx_loaded[0], b * 16 + 16)
                dve.wait_ge(ctx_loaded[1], b * 16 + 16)
                for i in range(2):
                    dve.bn_stats(ctx_stats[:, 6 * i:6 * i + 6], half(ctx_raw, i)).then_inc(ctx_step, 1)
                dve.wait_ge(ctx_step, b * 4 + 2)
                dve.sem_inc(waits_alone, 1)
                dve.bn_aggr(ctx_mean_var[:, :], ctx_stats[:, :]).then_inc(ctx_step, 1)
                dve.wait_ge(ctx_step, b * 4 + 3)
                dve.tensor_scalar(ctx_centred[:, :], ctx_raw[:, :], ctx_mean_var[:, 0:1], None, ALU.subtract)\
                   .then_inc(ctx_step, 1)

            def ctxT_low(b):
                for i in range(2):
                    c = slice(i * HC, (i + 1) * HC)
                    dve.wait_ge(ctxT_hi_done, b * 2 + i + 1)
                    dve.tensor_tensor(ctxT[:, c, M:2 * M], both_rows(tp_ps, i), ctxT[:, c, 0:M].bitcast(f32),
                                      ALU.subtract).then_inc(ctxT_split, 1)

            def ctx_low(b):
                dve.wait_ge(ctx_hi_done, b + 1)
                dve.tensor_tensor(ctx_lo[:, :], ctx_raw[:, :], ctx_hi[:, :].bitcast(f32),
                                  ALU.subtract).then_inc(ctx_split, 1)

            def norm_stats(tile, stats, mean_var, var_eps, steps, times):
                for i in range(2):
                    dve.bn_stats(stats[:, 6 * i:6 * i + 6], half(x[:, slot(tile), :], i)).then_inc(steps, 1)
                dve.wait_ge(steps, count(tile, 4, 2))
                dve.sem_inc(waits_alone, 1)
                dve.bn_aggr(mean_var[:, :], stats[:, :]).then_inc(steps, 1)
                dve.wait_ge(steps, count(tile, 4, 3))
                dve.tensor_scalar(var_eps[:, :], mean_var[:, 1:2], EPS, times, ALU.add, ALU.mult).then_inc(steps, 1)

            def norm1_stats(tile):
                b, j = tile
                dve.wait_ge(x_loaded[slot(tile)], b * (16 * TPB // XS) + 16 * (j // XS + 1))
                norm_stats(tile, stats1, mean_var1, var_eps1, ln1_step, SCALE ** -2)

            def xT_low(tile, i):
                dve.wait_ge(xT_hi_done, pairs(tile, 2, i + 1))
                dve.tensor_tensor(c_half(xT_lo, i), c_half(xT_raw[:, tile[1] // 2 % 2], i),
                                  c_half(xT_hi, i).bitcast(f32), ALU.subtract).then_inc(xT_split, 1)

            def softmax_scores(tile):
                b, j = tile
                if j % TPB == 0:
                    dve.wait_ge(mask_step, b * 3 + (j // TPB * 3 + 3))
                dve.wait_ge(rstd1_done, count(tile, 1, 1))
                dve.wait_ge(scores_done, count(tile, 1, 1))
                dve.scalar_tensor_tensor(out=s_part[:, :], in0=st_ps[:, M:2 * M], scalar=rstd1[:, :],
                                         in1=mask_bias[:, :], op0=ALU.mult, op1=ALU.add).then_inc(softmax_step, 1)
                dve.wait_ge(softmax_step, count(tile, 5, 1))
                dve.scalar_tensor_tensor(out=s_all[:, :], in0=st_ps[:, 0:M], scalar=rstd1[:, :],
                                         in1=s_part[:, :], op0=ALU.mult, op1=ALU.add).then_inc(softmax_step, 1)
                dve.wait_ge(softmax_step, count(tile, 5, 2))
                dve.tensor_reduce(out=neg_max[:, :], in_=s_all[:, :], axis=AX.X, op=ALU.max,
                                  negate=True).then_inc(softmax_step, 1)

            def softmax_split(tile):
                dve.wait_ge(exp_done, count(tile, 2, 2))
                dve.tensor_tensor(e_split[:, M:2 * M], e_all[:, :], e_split[:, 0:M].bitcast(f32),
                                  ALU.subtract).then_inc(e_split_done, 1)
                dve.reciprocal(e_inv[:, :], e_sum[:, :]).then_inc(softmax_step, 1)
                dve.wait_ge(softmax_step, count(tile, 5, 4))
                dve.tensor_tensor(e_scale[:, :], e_inv[:, :], any_valid[:, :], ALU.mult).then_inc(softmax_step, 1)

            def add_readout(tile):
                dve.wait_ge(softmax_step, count(tile, 5, 5))
                for i in range(2):
                    xh = half(x[:, slot(tile), :], i)
                    dve.wait_ge(readout_done, count(tile, 2, i + 1))
                    dve.scalar_tensor_tensor(out=xh, in0=half(ro_ps, i), scalar=e_scale[:, :], in1=xh,
                                             op0=ALU.mult, op1=ALU.add).then_inc(x1_done, 1)

            def norm2_stats(tile):
                dve.wait_ge(x1_done, count(tile, 2, 2))
                norm_stats(tile, stats2, mean_var2, var_eps2, ln2_step, 1.0)

            def norm2(tile):
                dve.wait_ge(rstd2_done, count(tile, 1, 1))
                dve.wait_ge(x2T_done, count(tile, 2))
                dve.tensor_scalar(xn2[:, :], x[:, slot(tile), :], mean_var2[:, 0:1], rstd2[:, :],
                                  ALU.subtract, ALU.mult).then_inc(xn2_done, 1)

            def x2T_low(tile):
                k = tile[1] % 2
                for i in range(2):
                    dve.wait_ge(x2T_hi_done, count(tile, 2, i + 1))
                    dve.tensor_tensor(chunks(xT2_lo[:, k], i), half(tp_ps, i), chunks(xT2_hi[:, k], i).bitcast(f32),
                                      ALU.subtract).then_inc(x2T_split, 1)

            def router_top(tile):
                logits = lr_ps[:, ER:LR]
                dve.wait_ge(lr_done, count(tile, 1, 1))
                dve.sem_inc(waits_alone, 1)
                dve.max(top8[:, :], logits).then_inc(router_step, 1)
                dve.wait_ge(router_step, count(tile, 9, 1))
                dve.sem_inc(waits_alone, 1)
                dve.max_index(top8_at[:, :], top8[:, :], logits).then_inc(router_step, 1)
                dve.wait_ge(router_step, count(tile, 9, 2))
                dve.tensor_copy(top2_at[:, :], top8_at[:, 0:2]).then_inc(router_step, 1)

            def router_gate(tile):
                dve.wait_ge(gate_exp_done, count(tile, 1, 1))
                dve.tensor_scalar_add(gate_den[:, :], gate_num[:, 1:2], 1.0).then_inc(router_step, 1)
                dve.wait_ge(router_step, count(tile, 9, 4))
                dve.reciprocal(gate_inv[:, :], gate_den[:, :]).then_inc(router_step, 1)
                dve.wait_ge(router_step, count(tile, 9, 5))
                dve.tensor_scalar(gate[:, :], gate_num[:, :], gate_inv[:, :], SCALING, ALU.mult, ALU.mult)\
                   .then_inc(router_step, 1)
                dve.wait_ge(router_step, count(tile, 9, 6))
                dve.tensor_scalar(gate_a[:, :], iota8[:, :], top2_at[:, 0:1], gate[:, 0:1], ALU.is_equal, ALU.mult)\
                   .then_inc(router_step, 1)
                dve.tensor_scalar(gate_b[:, :], iota8[:, :], top2_at[:, 1:2], gate[:, 1:2], ALU.is_equal, ALU.mult)\
                   .then_inc(router_step, 1)
                dve.wait_ge(router_step, count(tile, 9, 8))
                dve.tensor_tensor(w_dense[:, :], gate_a[:, :], gate_b[:, :], ALU.add).then_inc(router_step, 1)
                dve.wait_ge(router_step, count(tile, 9, 9))
                dve.tensor_tensor(h[:, :].rearrange("p (e r) -> p e r", r=R),
                                  lr_ps[:, 0:ER].rearrange("p (e r) -> p e r", r=R),
                                  w_dense[:, :].unsqueeze(2).to_broadcast([P, E, R]),
                                  ALU.mult).then_inc(h_done, 1)

            def hT_low(tile):
                dve.wait_ge(hT_hi_done, count(tile, 1, 1))
                dve.tensor_tensor(hT_lo[:, :], s_ps[:, 0:P], hT_hi[:, :].bitcast(f32),
                                  ALU.subtract).then_inc(hT_split, 1)

            def add_base(tile, g):
                o0, n = OUTS[g]
                xg = x[:, slot(tile), o0:o0 + n]
                dve.wait_ge(base_done, count(tile, G, g + 1))
                dve.tensor_tensor(xg, base_ps[g][:, 0:n], xg, ALU.add).then_inc(out_done, 1)

            def step(tile):
                b, j = tile
                nxt, nxt2 = after(tile, 1), after(tile, 2)
                if exists(nxt):
                    softmax_scores(nxt)
                if exists(nxt2):
                    norm1_stats(nxt2)
                if exists(nxt):
                    softmax_split(nxt)
                if exists(after(tile, 2 + j % 2)):
                    xT_low(after(tile, 2 + j % 2), 1 - j % 2)
                router_top(tile)
                router_gate(tile)
                if j == TPB - 3 and exists((b, TPB)):
                    ctxT_low(b + 1)
                if exists(nxt):
                    add_readout(nxt)
                    norm2_stats(nxt)
                hT_low(tile)
                if exists(nxt):
                    norm2(nxt)
                if j == TPB - 4 and exists((b, TPB)):
                    ctx_centre(b + 1)
                if exists(nxt):
                    x2T_low(nxt)
                for g in range(G):
                    if g == G - 1 and j == TPB - 2 and exists((b, TPB)):
                        ctx_low(b + 1)
                        mask(b + 1)
                    add_base(tile, g)

            dve.sem_inc(out_done, FREE)
            dve.wait_ge(constants_ready, E + 3)
            ctx_centre(0)
            xT_low((0, 0), 0)
            ctxT_low(0)
            xT_low((0, 0), 1)
            ctx_low(0)
            mask(0)
            norm1_stats((0, 0))
            w_low(dve, 0, 0)
            softmax_scores((0, 0))
            w_low(dve, 0, 1)
            softmax_split((0, 0))
            w_low(dve, 0, 2)
            w_low(dve, 0, 3)
            add_readout((0, 0))
            norm2_stats((0, 0))
            norm1_stats((0, 1))
            norm2((0, 0))
            w_low(dve, 1, 0)
            x2T_low((0, 0))
            xT_low((0, 2), 0)
            for r in range(1, WPARTS):
                w_low(dve, 1, r)
            dve.wait_ge(b_hi_done, 1)
            dve.tensor_tensor(b_lo[:, :], b_raw[:, :], b_hi[:, :].bitcast(f32), ALU.subtract).then_inc(b_split, 1)
            with dve.Fori(0, NB - 1) as b:
                for j in range(TPB):
                    step((b, j))
            for j in range(TPB):
                step((NB - 1, j))

        @block.tensor
        def _(pe):
            def three(out_, a_hi, a_lo, w_h, w_l, start, stop, again=False):
                pe.matmul(out_, a_hi, w_h, start=start, stop=False, skip_group_check=again)
                pe.matmul(out_, a_hi, w_l, start=False, stop=False, skip_group_check=again)
                return pe.matmul(out_, a_lo, w_h, start=False, stop=stop, skip_group_check=again)

            def transposes(ps_, src, done):
                for c in range(C):
                    mm = pe.transpose(ps_[:, c * P:(c + 1) * P], src[:, c * P:(c + 1) * P], ident[:, :])
                    if c % HC == HC - 1:
                        mm.then_inc(done, 1)

            def ctx_transposes(b):
                pe.wait_ge(ctx_step, b * 4 + 4)
                transposes(tp_ps, ctx_centred, ctxT_done)

            def pair_scores(tile):
                b, j = tile
                if j % TPB == 0:
                    pe.wait_ge(ctxT_split, b * 2 + (j // TPB * 2 + 2))
                pe.wait_ge(xT_split, pairs(tile, 2, 2))
                for c in range(C):
                    pe.matmul(s_ps[:, 0:T2], ctxT[:, c, :], xT_hi[:, c, :], start=(c == 0), stop=False)
                    mm = pe.matmul(s_ps[:, 0:T2], ctxT[:, c, :], xT_lo[:, c, :], start=False, stop=(c == C - 1))
                mm.then_inc(sT_done, 1)

            def scores(tile):
                k = tile[1] % 2
                pe.wait_ge(sT_copied, pairs(tile, 1, 1))
                pe.wait_ge(x1_done, count(tile, 2))
                pe.transpose(st_ps, sT[:, k * P:(k + 1) * P], ident[:, :]).then_inc(scores_done, 1)

            def e_transpose(tile):
                pe.wait_ge(e_split_done, count(tile, 1, 1))
                pe.transpose(et_ps, e_split[:, :].bitcast(f32), ident[:, :]).then_inc(eT_done, 1)

            def readout(tile):
                b, j = tile
                if j % TPB == 0:
                    pe.wait_ge(ctx_split, b + j // TPB + 1)
                pe.wait_ge(eT_copied, count(tile, 1, 1))
                for i in range(2):
                    pe.matmul(half(ro_ps, i), eT[:, :], half(ctx_hi, i), start=True, stop=False)
                    pe.matmul(half(ro_ps, i), eT[:, :], half(ctx_lo, i), start=False, stop=True)\
                      .then_inc(readout_done, 1)

            def x2_transposes(tile):
                pe.wait_ge(xn2_done, count(tile, 1, 1))
                pe.wait_ge(x2T_split, count(tile, 2))
                transposes(tp_ps, xn2, x2T_done)

            def base(tile, g, chunks_):
                k = tile[1] % 2
                ps_ = base_ps[g][:, 0:GROUPS[g][1]]
                if chunks_[0] == 0:
                    if tile[1] == 0:
                        pe.wait_ge(w_split[g], WPARTS)
                    pe.wait_ge(out_done, count(tile, G, g + 1))
                for c in chunks_:
                    mm = three(ps_, xT2_hi[:, k, c, :], xT2_lo[:, k, c, :], w_columns(w_hi, g)[:, c, :],
                               w_columns(w_lo, g)[:, c, :], c == 0, g == 0 and c == C - 1)
                if g == 0 and c == C - 1:
                    mm.then_inc(lr_done, 1)

            def h_transpose(tile):
                pe.wait_ge(h_done, count(tile, 1, 1))
                pe.transpose(s_ps[:, 0:P], h[:, :], ident[:, :]).then_inc(hT_done, 1)

            def lora_second(tile, g):
                o0, n = OUTS[g]
                if tile[1] == 0:
                    pe.wait_ge(b_split, 1)
                pe.wait_ge(hT_split, count(tile, 1, 1))
                three(base_ps[g][:, 0:n], hT_hi[:, :], hT_lo[:, :], b_hi[:, o0:o0 + n], b_lo[:, o0:o0 + n],
                      False, True, again=(g == 0)).then_inc(base_done, 1)

            def step(tile):
                b, j = tile
                nxt, nxt2 = after(tile, 1), after(tile, 2)
                if exists(nxt):
                    scores(nxt)
                pe.wait_ge(x2T_split, count(tile, 2, 2))
                base(tile, 0, range(C))
                if exists(nxt):
                    e_transpose(nxt)
                base(tile, 1, range(3))
                if j == TPB - 3 and exists((b, TPB)):
                    ctx_transposes(b + 1)
                if exists(nxt):
                    readout(nxt)
                base(tile, 1, range(3, C))
                h_transpose(tile)
                base(tile, 2, range(6))
                if exists(nxt):
                    if j == TPB - 3 and exists((b, TPB)):
                        pe.wait_ge(ctxT_split, b * 2 + 4)
                    x2_transposes(nxt)
                lora_second(tile, 0)
                lora_second(tile, 1)
                if j % 2 == 0 and exists(nxt2):
                    pair_scores(nxt2)
                base(tile, 2, range(6, C))
                lora_second(tile, 2)

            pe.wait_ge(constants_ready, E + 3)
            ctx_transposes(0)
            pair_scores((0, 0))
            scores((0, 0))
            e_transpose((0, 0))
            readout((0, 0))
            pe.wait_ge(ctxT_split, 2)
            x2_transposes((0, 0))
            with pe.Fori(0, NB - 1) as b:
                for j in range(TPB):
                    step((b, j))
            for j in range(TPB):
                step((NB - 1, j))


def kernel(x, ctx_2048, mask_BxS2_bk0, L0_ffn_weight, L0_ffn_lora_A, L0_ffn_lora_B, L0_ffn_router_w):
    import numpy as np
    import concourse.bacc as bacc
    from concourse import mybir as mb
    from concourse.bass_utils import run_bass_kernel_spmd

    P = 128

    def by_contraction(a):
        n, d = a.shape
        return np.ascontiguousarray(a.T.reshape(d // P, P, n).transpose(1, 0, 2))

    x, ctx, mask = np.asarray(x), np.asarray(ctx_2048), np.asarray(mask_BxS2_bk0)
    weight, lora_a, lora_b, router = (
        np.asarray(a) for a in (L0_ffn_weight, L0_ffn_lora_A, L0_ffn_lora_B, L0_ffn_router_w))
    B, S, D = x.shape
    E, R, _ = lora_a.shape
    O = weight.shape[0]
    w0 = O - 2 * ((O + E * R + E) // 6 * 2)
    arrays = {
        "x": np.ascontiguousarray(x.reshape(B * S // P, P, D)),
        "xT": np.stack([by_contraction(rows) for rows in x.reshape(B * S // (2 * P), 2 * P, D)]),
        "ctx": np.ascontiguousarray(ctx),
        "mask": np.ascontiguousarray(mask),
        "wT": by_contraction(np.concatenate([weight[:w0], lora_a.reshape(E * R, D), router, weight[w0:]])),
        "bT": np.ascontiguousarray(lora_b.transpose(0, 2, 1).reshape(E * R, O)),
    }
    nc = bacc.Bacc("TRN2", target_bir_lowering=False, num_devices=1)
    args = [nc.dram_tensor(f"in_{n}", a.shape, mb.dt.from_np(a.dtype), kind="ExternalInput").ap()
            for n, a in arrays.items()]
    out = nc.dram_tensor("out", (B * S // P, P, O), mb.dt.float32, kind="ExternalOutput").ap()
    xattn_lora_moe_kernel(nc, *args, out)
    r = run_bass_kernel_spmd(nc, [{f"in_{n}": a for n, a in arrays.items()}], core_ids=[0])
    return r.results[0]["out"].reshape(B, S, O)
```

```python
import concourse.bass as bass
from concourse import mybir
from contextlib import ExitStack


def xattn_lora_moe_kernel(
    nc: bass.Bass,
    x_in: bass.AP,
    xT_in: bass.AP,
    ctx_in: bass.AP,
    ctxT_in: bass.AP,
    mask_in: bass.AP,
    wT_in: bass.AP,
    bT_in: bass.AP,
    out: bass.AP,
):
    f32 = mybir.dt.float32
    f32r = mybir.dt.float32r
    u8 = mybir.dt.uint8
    u32 = mybir.dt.uint32
    ALU = mybir.AluOpType
    ACT = mybir.ActivationFunctionType
    AX = mybir.AxisListType

    P = 128
    NT, _, D = x_in.shape
    NB, M, _ = ctx_in.shape
    ER, O = bT_in.shape
    WC = wT_in.shape[2]
    LR = WC - O
    E = LR - ER
    R = ER // E
    C = D // P
    HC = C // 2
    H = 512
    TPB = NT // NB
    T2 = 2 * P
    XS = 4
    Q = 4
    QP = P // Q
    DQ = D // Q
    DVE_Q = 1
    ACT_Q = Q - DVE_Q
    EPS = 1e-5
    SCALING = 2.0
    SCALE = float(D) ** -0.5
    MASKED = 1e30
    assert D == 2 * H and O == 2 * H and M * 2 == P and ER == P and TPB % XS == 0
    SIDE = WC // 6 * 2
    W0 = O - 2 * SIDE
    GROUPS = [(0, W0 + LR), (W0 + LR, SIDE), (W0 + LR + SIDE, SIDE)]
    OUTS = [(0, W0), (W0, SIDE), (W0 + SIDE, SIDE)]
    G = len(GROUPS)
    WPARTS = 4
    CP = C // WPARTS

    def count(tile, per, more=0):
        b, j = tile
        return b * (TPB * per) + (j * per + more)

    def after(tile, n):
        return (tile[0], tile[1] + n)

    def exists(tile):
        return not isinstance(tile[0], int) or tile[0] * TPB + tile[1] < NT

    def slot(tile):
        return tile[1] % XS

    def pairs(tile, per, more=0):
        b, j = tile
        return b * (TPB // 2 * per) + (j // 2 * per + more)

    stack = ExitStack()
    with stack:
        def sb(name, shape, dt=f32):
            return stack.enter_context(nc.sbuf_tensor(name, shape, dt))

        def ps(name, shape):
            return stack.enter_context(nc.psum_tensor(name, shape, f32))

        def sem(name):
            return stack.enter_context(nc.semaphore(name))

        w_hi = sb("w_hi", [P, C, WC], f32r)
        w_lo = sb("w_lo", [P, C, WC], f32r)
        b_hi = sb("b_hi", [P, O], f32r)
        b_lo = sb("b_lo", [P, O], f32r)
        w_raw = [sb(f"w_raw{i}", [P, C, GROUPS[0][1]]) for i in range(2)]
        b_raw = sb("b_raw", [P, O])
        ctxT = sb("ctxT", [P, C, 2 * M], f32r)
        ctx_hi = sb("ctx_hi", [P, D], f32r)
        ctx_lo = sb("ctx_lo", [P, D], f32r)
        ctx_raw = sb("ctx_raw", [P, D])
        ctxT_raw = sb("ctxT_raw", [P, C, M])
        ctxT_centred = sb("ctxT_centred", [P, C, M])
        ctx_sum = sb("ctx_sum", [P, M])
        mask_raw = sb("mask_raw", [P, M], u8)
        mask_f = sb("mask_f", [P, M])
        mask_bias = sb("mask_bias", [P, M])
        any_valid = sb("any_valid", [P, 1])
        x = sb("x", [P, XS, D])
        xn2 = sb("xn2", [P, Q, DQ])
        xT_raw = sb("xT_raw", [P, 2, C, T2])
        xT_hi = sb("xT_hi", [P, C, T2], f32r)
        xT_lo = sb("xT_lo", [P, C, T2], f32r)
        sT = sb("sT", [P, T2])
        x2T = sb("x2T", [P, C, P])
        xT2_hi = sb("xT2_hi", [P, 2, C, P], f32r)
        xT2_lo = sb("xT2_lo", [P, 2, C, P], f32r)
        ident = sb("ident", [P, P])
        one_dth = sb("one_dth", [P, P])
        iota8 = sb("iota8", [P, E])
        neg_half = sb("neg_half", [P, 1])
        stats1 = sb("stats1", [P, 12])
        mean_var1 = sb("mean_var1", [P, 2])
        var_eps1 = sb("var_eps1", [P, 1])
        rstd1 = sb("rstd1", [P, 1])
        stats2 = sb("stats2", [P, 12])
        mean_var2 = sb("mean_var2", [P, 2])
        var_eps2 = sb("var_eps2", [P, 1])
        rstd2 = sb("rstd2", [P, 1])
        neg_mean2 = sb("neg_mean2", [P, 1])
        shift2 = sb("shift2", [P, 1])
        s_part = sb("s_part", [P, M])
        s_all = sb("s_all", [P, M])
        neg_max = sb("neg_max", [P, 1])
        e_all = sb("e_all", [P, M])
        e_split = sb("e_split", [P, 2 * M], f32r)
        e_sum = sb("e_sum", [P, 1])
        e_inv = sb("e_inv", [P, 1])
        e_scale = sb("e_scale", [P, 1])
        eT = sb("eT", [P, P], f32r)
        top8 = sb("top8", [P, 8])
        top8_at = sb("top8_at", [P, 8], u32)
        top2_at = sb("top2_at", [P, 2])
        gate_num = sb("gate_num", [P, 2])
        gate_den = sb("gate_den", [P, 1])
        gate_inv = sb("gate_inv", [P, 1])
        gate = sb("gate", [P, 2])
        gate_a = sb("gate_a", [P, E])
        gate_b = sb("gate_b", [P, E])
        w_dense = sb("w_dense", [P, E])
        h = sb("h", [P, ER])
        hT_hi = sb("hT_hi", [P, P], f32r)
        hT_lo = sb("hT_lo", [P, P], f32r)

        base_ps = [[ps(f"base_ps{g}_{k}", [P, H]) for k in range(2 if g == 0 else 1)] for g in range(G)]
        s_ps = ps("s_ps", [P, H])
        h_ps = ps("h_ps", [P, H])
        ro_ps = ps("ro_ps", [P, D])
        st_ps = ro_ps[:, 0:2 * M]
        et_ps = ro_ps[:, H:H + P]

        def base_bank(tile, g):
            return base_ps[g][tile[1] % len(base_ps[g])]

        def lr_ps(tile):
            return base_bank(tile, 0)[:, W0:W0 + LR]

        def half(t, i):
            return t[:, i * H:(i + 1) * H]

        def chunks(t, i):
            return t[:, i * HC:(i + 1) * HC, :].rearrange("p c n -> p (c n)")

        def c_half(t, i):
            return t[:, i * HC:(i + 1) * HC, :]

        def w_columns(t, g):
            c0, n = GROUPS[g]
            return t[:, :, c0:c0 + n]

        def w_part(t, g, r):
            return w_columns(t, g)[:, r * CP:(r + 1) * CP, :]

        def raw_part(g, r):
            return w_raw[g % 2][:, r * CP:(r + 1) * CP, 0:GROUPS[g][1]]

        x_loaded = [sem(f"x_loaded{s}") for s in range(XS)]
        stored = [sem(f"stored{s}") for s in range(XS)]
        xT_loaded = [[sem(f"xT_loaded{k}_{i}") for i in range(2)] for k in range(2)]
        ctxT_loaded = sem("ctxT_loaded")
        ctx_loaded = [sem(f"ctx_loaded{i}") for i in range(3)]
        w_loaded = [sem(f"w_loaded{g}") for g in range(G)]
        b_loaded = sem("b_loaded")
        CONSTANTS = E + 4
        constants_ready = sem("constants_ready")
        ident_zeroed = sem("ident_zeroed")
        waits_alone = sem("waits_alone")
        w_hi_done = [sem(f"w_hi_done{g}") for g in range(G)]
        w_split = [sem(f"w_split{g}") for g in range(G)]
        b_hi_done = sem("b_hi_done")
        b_split = sem("b_split")
        ctx_sum_done = sem("ctx_sum_done")
        ctx_mean_done = sem("ctx_mean_done")
        ctx_centred = sem("ctx_centred")
        ctxT_hi_done = sem("ctxT_hi_done")
        ctxT_split = sem("ctxT_split")
        ctx_hi_done = sem("ctx_hi_done")
        ctx_split = sem("ctx_split")
        mask_step = sem("mask_step")
        ln1_step = sem("ln1_step")
        rstd1_done = sem("rstd1_done")
        xT_hi_done = sem("xT_hi_done")
        xT_split = sem("xT_split")
        sT_done = sem("sT_done")
        sT_copied = sem("sT_copied")
        scores_done = sem("scores_done")
        softmax_step = sem("softmax_step")
        exp_done = sem("exp_done")
        e_split_done = sem("e_split_done")
        eT_done = sem("eT_done")
        eT_copied = sem("eT_copied")
        readout_done = sem("readout_done")
        x1_done = sem("x1_done")
        ln2_step = sem("ln2_step")
        rstd2_done = sem("rstd2_done")
        neg_mean2_done = sem("neg_mean2_done")
        shift2_done = sem("shift2_done")
        xn2_act_done = sem("xn2_act_done")
        xn2_dve_done = sem("xn2_dve_done")
        x2T_done = sem("x2T_done")
        x2T_hi_done = sem("x2T_hi_done")
        x2T_split = sem("x2T_split")
        lr_done = sem("lr_done")
        router_step = sem("router_step")
        gate_exp_done = sem("gate_exp_done")
        h_done = sem("h_done")
        hT_done = sem("hT_done")
        hT_hi_done = sem("hT_hi_done")
        hT_split = sem("hT_split")
        base_done = sem("base_done")
        FREE = 2 * G
        out_done = sem("out_done")

        block = stack.enter_context(nc.Block())

        def w_low(engine, g, r):
            engine.wait_ge(w_hi_done[g], r + 1)
            engine.tensor_tensor(w_part(w_lo, g, r), raw_part(g, r), w_part(w_hi, g, r).bitcast(f32),
                                 ALU.subtract).then_inc(w_split[g], 1)

        @block.sync
        def _(sp):
            def load_x(tile):
                b, j = tile
                sp.dma_start(x[:, slot(tile), :], x_in[b * TPB + j]).then_inc(x_loaded[slot(tile)], 16)

            def load_xT(tile):
                b, j = tile
                k = j // 2 % 2
                for i in range(2):
                    sp.dma_start(c_half(xT_raw[:, k], i), c_half(xT_in[b * (TPB // 2) + j // 2], i))\
                      .then_inc(xT_loaded[k][i], 16)

            def load_ctx(b):
                sp.dma_start(ctx_raw[0:M, :], ctx_in[b]).then_inc(ctx_loaded[0], 16)
                sp.dma_start(ctx_raw[M:P, :], ctx_in[b]).then_inc(ctx_loaded[1], 16)
                sp.dma_start(mask_raw[:, :], mask_in[b].partition_broadcast(P)).then_inc(ctx_loaded[2], 16)

            def load_w(g):
                c0, n = GROUPS[g]
                sp.dma_start(w_raw[g % 2][:, :, 0:n], wT_in[:, :, c0:c0 + n]).then_inc(w_loaded[g], 16)

            def load_ctxT(b):
                sp.dma_start(ctxT_raw[:, :, :], ctxT_in[b]).then_inc(ctxT_loaded, 16)

            load_ctxT(0)
            load_xT((0, 0))
            load_x((0, 0))
            load_ctx(0)
            load_w(0)
            load_x((0, 1))
            load_xT((0, 2))
            load_w(1)
            sp.dma_start(b_raw[:, :], bT_in).then_inc(b_loaded, 16)
            sp.wait_ge(w_split[0], WPARTS)
            load_w(2)
            load_x((0, 2))
            load_x((0, 3))

            def step(tile):
                b, j = tile
                if j % 2 == 0 and exists(after(tile, 4)):
                    sp.wait_ge(xT_split, pairs(tile, 2, 2))
                    load_xT(after(tile, 4))
                sp.wait_ge(out_done, count(tile, G, FREE + G))
                sp.dma_start(out[b * TPB + j], x[:, slot(tile), :]).then_inc(stored[slot(tile)], 16)
                if exists(after(tile, XS)):
                    sp.wait_ge(stored[slot(tile)], b * (16 * TPB // XS) + 16 * (j // XS + 1))
                    load_x(after(tile, XS))
                if j == 0 and exists((b, TPB)):
                    sp.wait_ge(ctx_split, b + 1)
                    sp.wait_ge(mask_step, b * 3 + 3)
                    load_ctx(b + 1)
                    sp.wait_ge(ctx_centred, b + 1)
                    load_ctxT(b + 1)

            with sp.Fori(0, NB - 1) as b:
                for j in range(TPB):
                    step((b, j))
            for j in range(TPB):
                step((NB - 1, j))
            for s in range(XS):
                sp.wait_ge(stored[s], 16 * NT // XS)

        @block.gpsimd
        def _(pool):
            pool.memset(ident[:, :], 0.0).then_inc(ident_zeroed, 1)
            pool.wait_ge(ident_zeroed, 1)
            pool.affine_select(out=ident[:, :], in_=ident[:, :], compare_op=ALU.not_equal, fill=1.0,
                               base=0, pattern=[[-1, P]], channel_multiplier=1).then_inc(constants_ready, 1)
            for e in range(E):
                pool.memset(iota8[:, e:e + 1], float(e)).then_inc(constants_ready, 1)
            pool.memset(gate_num[:, 0:1], 1.0).then_inc(constants_ready, 1)
            pool.memset(neg_half[:, :], -0.5).then_inc(constants_ready, 1)
            pool.wait_ge(constants_ready, CONSTANTS - 1)

            def rstd(tile, var_eps, out_, steps, done):
                pool.wait_ge(steps, count(tile, 4, 4))
                pool.tensor_tensor(out_[:, :], var_eps[:, :], neg_half[:, :], ALU.pow).then_inc(done, 1)

            def ctx_low(b):
                pool.wait_ge(ctx_hi_done, b + 1)
                pool.tensor_tensor(ctx_lo[:, :], ctx_raw[:, :], ctx_hi[:, :].bitcast(f32),
                                   ALU.subtract).then_inc(ctx_split, 1)

            def norm1(tile):
                rstd(tile, var_eps1, rstd1, ln1_step, rstd1_done)

            def norm2(tile):
                rstd(tile, var_eps2, rstd2, ln2_step, rstd2_done)
                pool.wait_ge(neg_mean2_done, count(tile, 1, 1))
                pool.wait_ge(rstd2_done, count(tile, 1, 1))
                pool.tensor_tensor(shift2[:, :], neg_mean2[:, :], rstd2[:, :], ALU.mult).then_inc(shift2_done, 1)

            def xT_low(tile, i):
                pool.wait_ge(xT_hi_done, pairs(tile, 2, i + 1))
                pool.tensor_tensor(c_half(xT_lo, i), c_half(xT_raw[:, tile[1] // 2 % 2], i),
                                   c_half(xT_hi, i).bitcast(f32), ALU.subtract).then_inc(xT_split, 1)

            def step(tile):
                b, j = tile
                if j == TPB - 2 and exists((b, TPB)):
                    ctx_low(b + 1)
                if j % 2 == 1 and exists(after(tile, 3)):
                    for i in range(2):
                        xT_low(after(tile, 3), i)
                if exists(after(tile, 2)):
                    norm1(after(tile, 2))
                    norm2(after(tile, 2))

            norm1((0, 0))
            ctx_low(0)
            for r in range(2, WPARTS):
                w_low(pool, 0, r)
            norm2((0, 0))
            norm1((0, 1))
            for i in range(2):
                xT_low((0, 2), i)
            pool.wait_ge(b_loaded, 16)
            pool.tensor_copy(b_hi[:, :], b_raw[:, :]).then_inc(b_hi_done, 1)
            pool.wait_ge(b_hi_done, 1)
            pool.tensor_tensor(b_lo[:, :], b_raw[:, :], b_hi[:, :].bitcast(f32), ALU.subtract).then_inc(b_split, 1)
            norm2((0, 1))
            for r in range(WPARTS):
                w_low(pool, G - 1, r)
            with pool.Fori(0, NB - 1) as b:
                for j in range(TPB):
                    step((b, j))
            for j in range(TPB):
                step((NB - 1, j))

        @block.scalar
        def _(act):
            def ctxT_high(b):
                act.wait_ge(ctx_centred, b + 1)
                act.copy(ctxT[:, :, 0:M], ctxT_centred[:, :, :]).then_inc(ctxT_hi_done, 1)

            def ctx_high(b):
                act.wait_ge(ctx_loaded[0], b * 16 + 16)
                act.wait_ge(ctx_loaded[1], b * 16 + 16)
                act.wait_ge(readout_done, count((b, 0), 2))
                act.copy(ctx_hi[:, :], ctx_raw[:, :]).then_inc(ctx_hi_done, 1)

            def xT_high(tile, i):
                b, j = tile
                k = j // 2 % 2
                act.wait_ge(xT_loaded[k][i], b * (16 * TPB // 4) + 16 * (j // 4 + 1))
                act.wait_ge(sT_done, pairs(tile, 1))
                act.copy(c_half(xT_hi, i), c_half(xT_raw[:, k], i)).then_inc(xT_hi_done, 1)

            def sT_copy(tile):
                act.wait_ge(sT_done, pairs(tile, 1, 1))
                act.wait_ge(scores_done, count(tile, 1))
                act.copy(sT[:, :], s_ps[:, 0:T2]).then_inc(sT_copied, 1)

            def softmax_exp(tile):
                act.wait_ge(softmax_step, count(tile, 5, 3))
                act.wait_ge(e_split_done, count(tile, 1))
                act.wait_ge(x1_done, count(tile, 2))
                act.wait_ge(eT_done, count(tile, 1))
                act.activation(e_all[:, :], s_all[:, :], ACT.Exp, bias=neg_max[:, :],
                               accum_out=e_sum[:, :]).then_inc(exp_done, 1)
                act.activation(e_split[:, 0:M], s_all[:, :], ACT.Exp, bias=neg_max[:, :]).then_inc(exp_done, 1)

            def eT_copy(tile):
                act.wait_ge(eT_done, count(tile, 1, 1))
                act.wait_ge(readout_done, count(tile, 2))
                act.copy(eT[:, :], et_ps).then_inc(eT_copied, 1)

            def norm2(tile, g):
                rows = slice(g * QP, (g + 1) * QP)
                if g == 0:
                    act.wait_ge(shift2_done, count(tile, 1, 1))
                for a in range(DVE_Q, Q):
                    act.activation(xn2[a * QP:(a + 1) * QP, g, :], x[rows, slot(tile), a * DQ:(a + 1) * DQ],
                                   ACT.Identity, bias=shift2[rows, :], scale=rstd2[rows, :]).then_inc(xn2_act_done, 1)

            def x2T_high(tile):
                act.wait_ge(x2T_done, count(tile, Q, Q))
                for i in range(2):
                    act.copy(chunks(xT2_hi[:, tile[1] % 2], i), chunks(x2T, i)).then_inc(x2T_hi_done, 1)

            def gate_exp(tile):
                act.wait_ge(router_step, count(tile, 9, 1))
                act.activation(gate_num[:, 1:2], top8[:, 0:1], ACT.Exp, bias=top8[:, 1:2],
                               scale=-1.0).then_inc(gate_exp_done, 1)

            def hT_high(tile):
                act.wait_ge(hT_done, count(tile, 1, 1))
                act.copy(hT_hi[:, :], h_ps[:, 0:P]).then_inc(hT_hi_done, 1)

            def w_high(g, r):
                act.wait_ge(w_loaded[g], 16)
                act.copy(w_part(w_hi, g, r), raw_part(g, r)).then_inc(w_hi_done[g], 1)

            def step(tile):
                b, j = tile
                nxt, nxt2 = after(tile, 1), after(tile, 2)
                if j % 2 == 1 and exists(after(tile, 3)):
                    for i in range(2):
                        xT_high(after(tile, 3), i)
                if j == TPB - 2 and exists((b, TPB)):
                    ctx_high(b + 1)
                for g in range(Q):
                    if exists(nxt):
                        norm2(nxt, g)
                    if g == 1:
                        gate_exp(tile)
                        if j % 2 == 0 and exists(nxt2):
                            sT_copy(nxt2)
                if exists(nxt2):
                    softmax_exp(nxt2)
                if j == TPB - 3 and exists((b, TPB)):
                    ctxT_high(b + 1)
                hT_high(tile)
                if exists(nxt2):
                    eT_copy(nxt2)
                if exists(nxt):
                    x2T_high(nxt)

            act.wait_ge(constants_ready, CONSTANTS - 1)
            act.activation(one_dth[:, :], ident[:, :], ACT.Copy, bias=1.0 / D, scale=0.0).then_inc(constants_ready, 1)
            act.wait_ge(constants_ready, CONSTANTS)
            ctxT_high(0)
            for i in range(2):
                xT_high((0, 0), i)
            ctx_high(0)
            sT_copy((0, 0))
            softmax_exp((0, 0))
            w_high(0, 0)
            eT_copy((0, 0))
            for r in range(1, WPARTS):
                w_high(0, r)
            for i in range(2):
                xT_high((0, 2), i)
            for g in range(Q):
                norm2((0, 0), g)
                if g == 1:
                    softmax_exp((0, 1))
            eT_copy((0, 1))
            x2T_high((0, 0))
            for g in range(1, G):
                for r in range(WPARTS):
                    w_high(g, r)
            with act.Fori(0, NB - 1) as b:
                for j in range(TPB):
                    step((b, j))
            for j in range(TPB):
                step((NB - 1, j))

        @block.vector
        def _(dve):
            def mask(b):
                dve.wait_ge(ctx_loaded[2], b * 16 + 16)
                dve.tensor_copy(mask_f[:, :], mask_raw[:, :]).then_inc(mask_step, 1)
                dve.wait_ge(mask_step, b * 3 + 1)
                dve.tensor_scalar(mask_bias[:, :], mask_f[:, :], -1.0, MASKED, ALU.add, ALU.mult)\
                   .then_inc(mask_step, 1)
                dve.reduce_max(any_valid[:, :], mask_f[:, :], AX.X).then_inc(mask_step, 1)

            def ctx_sum_chunks(b):
                dve.wait_ge(ctxT_loaded, b * 16 + 16)
                dve.tensor_reduce(out=ctx_sum[:, :], in_=ctxT_raw[:, :, :].rearrange("p c m -> p m c"), axis=AX.X,
                                  op=ALU.add).then_inc(ctx_sum_done, 1)

            def ctx_centre(b):
                dve.wait_ge(ctx_mean_done, b + 1)
                dve.tensor_tensor(ctxT_centred[:, :, :], ctxT_raw[:, :, :],
                                  h_ps[:, P:P + M].unsqueeze(1).to_broadcast([P, C, M]),
                                  ALU.subtract).then_inc(ctx_centred, 1)

            def ctxT_low(b):
                dve.wait_ge(ctxT_hi_done, b + 1)
                dve.tensor_tensor(ctxT[:, :, M:2 * M], ctxT_centred[:, :, :], ctxT[:, :, 0:M].bitcast(f32),
                                  ALU.subtract).then_inc(ctxT_split, 1)

            def norm_stats(tile, stats, mean_var, var_eps, steps, times):
                for i in range(2):
                    dve.bn_stats(stats[:, 6 * i:6 * i + 6], half(x[:, slot(tile), :], i)).then_inc(steps, 1)
                dve.wait_ge(steps, count(tile, 4, 2))
                dve.sem_inc(waits_alone, 1)
                dve.bn_aggr(mean_var[:, :], stats[:, :]).then_inc(steps, 1)
                dve.wait_ge(steps, count(tile, 4, 3))
                dve.tensor_scalar(var_eps[:, :], mean_var[:, 1:2], EPS, times, ALU.add, ALU.mult).then_inc(steps, 1)

            def norm1_stats(tile):
                b, j = tile
                dve.wait_ge(x_loaded[slot(tile)], b * (16 * TPB // XS) + 16 * (j // XS + 1))
                norm_stats(tile, stats1, mean_var1, var_eps1, ln1_step, SCALE ** -2)

            def xT_low(tile, i):
                dve.wait_ge(xT_hi_done, pairs(tile, 2, i + 1))
                dve.tensor_tensor(c_half(xT_lo, i), c_half(xT_raw[:, tile[1] // 2 % 2], i),
                                  c_half(xT_hi, i).bitcast(f32), ALU.subtract).then_inc(xT_split, 1)

            def softmax_scores(tile):
                b, j = tile
                if j % TPB == 0:
                    dve.wait_ge(mask_step, b * 3 + (j // TPB * 3 + 3))
                dve.wait_ge(rstd1_done, count(tile, 1, 1))
                dve.wait_ge(scores_done, count(tile, 1, 1))
                dve.scalar_tensor_tensor(out=s_part[:, :], in0=st_ps[:, M:2 * M], scalar=rstd1[:, :],
                                         in1=mask_bias[:, :], op0=ALU.mult, op1=ALU.add).then_inc(softmax_step, 1)
                dve.wait_ge(softmax_step, count(tile, 5, 1))
                dve.scalar_tensor_tensor(out=s_all[:, :], in0=st_ps[:, 0:M], scalar=rstd1[:, :],
                                         in1=s_part[:, :], op0=ALU.mult, op1=ALU.add).then_inc(softmax_step, 1)
                dve.wait_ge(softmax_step, count(tile, 5, 2))
                dve.tensor_reduce(out=neg_max[:, :], in_=s_all[:, :], axis=AX.X, op=ALU.max,
                                  negate=True).then_inc(softmax_step, 1)

            def softmax_split(tile):
                dve.wait_ge(exp_done, count(tile, 2, 2))
                dve.tensor_tensor(e_split[:, M:2 * M], e_all[:, :], e_split[:, 0:M].bitcast(f32),
                                  ALU.subtract).then_inc(e_split_done, 1)
                dve.reciprocal(e_inv[:, :], e_sum[:, :]).then_inc(softmax_step, 1)
                dve.wait_ge(softmax_step, count(tile, 5, 4))
                dve.tensor_tensor(e_scale[:, :], e_inv[:, :], any_valid[:, :], ALU.mult).then_inc(softmax_step, 1)

            def add_readout(tile):
                dve.wait_ge(softmax_step, count(tile, 5, 5))
                for i in range(2):
                    xh = half(x[:, slot(tile), :], i)
                    dve.wait_ge(readout_done, count(tile, 2, i + 1))
                    dve.scalar_tensor_tensor(out=xh, in0=half(ro_ps, i), scalar=e_scale[:, :], in1=xh,
                                             op0=ALU.mult, op1=ALU.add).then_inc(x1_done, 1)

            def norm2_stats(tile):
                dve.wait_ge(x1_done, count(tile, 2, 2))
                norm_stats(tile, stats2, mean_var2, var_eps2, ln2_step, 1.0)
                dve.tensor_scalar(neg_mean2[:, :], mean_var2[:, 0:1], -1.0, None, ALU.mult).then_inc(neg_mean2_done, 1)

            def norm2(tile, g):
                rows = slice(g * QP, (g + 1) * QP)
                if g == 0:
                    dve.wait_ge(rstd2_done, count(tile, 1, 1))
                for a in range(DVE_Q):
                    dve.tensor_scalar(xn2[a * QP:(a + 1) * QP, g, :], x[rows, slot(tile), a * DQ:(a + 1) * DQ],
                                      mean_var2[rows, 0:1], rstd2[rows, :], ALU.subtract, ALU.mult)\
                       .then_inc(xn2_dve_done, 1)

            def x2_transposes(tile, quadrants):
                for g in quadrants:
                    dve.wait_ge(xn2_dve_done, count(tile, Q * DVE_Q, DVE_Q * (g + 1)))
                    dve.wait_ge(xn2_act_done, count(tile, Q * ACT_Q, ACT_Q * (g + 1)))
                    dve.transpose(x2T[:, :, g * QP:(g + 1) * QP], xn2[:, g, :].rearrange("p (c n) -> p c n", n=QP))\
                       .then_inc(x2T_done, 1)

            def x2T_low(tile):
                k = tile[1] % 2
                for i in range(2):
                    dve.wait_ge(x2T_hi_done, count(tile, 2, i + 1))
                    dve.tensor_tensor(chunks(xT2_lo[:, k], i), chunks(x2T, i), chunks(xT2_hi[:, k], i).bitcast(f32),
                                      ALU.subtract).then_inc(x2T_split, 1)

            def router_top(tile):
                logits = lr_ps(tile)[:, ER:LR]
                dve.wait_ge(lr_done, count(tile, 1, 1))
                dve.sem_inc(waits_alone, 1)
                dve.max(top8[:, :], logits).then_inc(router_step, 1)
                dve.wait_ge(router_step, count(tile, 9, 1))
                dve.sem_inc(waits_alone, 1)
                dve.max_index(top8_at[:, :], top8[:, :], logits).then_inc(router_step, 1)
                dve.wait_ge(router_step, count(tile, 9, 2))
                dve.tensor_copy(top2_at[:, :], top8_at[:, 0:2]).then_inc(router_step, 1)

            def router_gate(tile):
                nxt = after(tile, 1)
                dve.wait_ge(gate_exp_done, count(tile, 1, 1))
                dve.tensor_scalar_add(gate_den[:, :], gate_num[:, 1:2], 1.0).then_inc(router_step, 1)
                if exists(nxt):
                    norm2(nxt, 2)
                dve.wait_ge(router_step, count(tile, 9, 4))
                dve.reciprocal(gate_inv[:, :], gate_den[:, :]).then_inc(router_step, 1)
                if exists(nxt):
                    norm2(nxt, 3)
                dve.wait_ge(router_step, count(tile, 9, 5))
                dve.tensor_scalar(gate[:, :], gate_num[:, :], gate_inv[:, :], SCALING, ALU.mult, ALU.mult)\
                   .then_inc(router_step, 1)
                dve.wait_ge(router_step, count(tile, 9, 6))
                dve.tensor_scalar(gate_a[:, :], iota8[:, :], top2_at[:, 0:1], gate[:, 0:1], ALU.is_equal, ALU.mult)\
                   .then_inc(router_step, 1)
                dve.tensor_scalar(gate_b[:, :], iota8[:, :], top2_at[:, 1:2], gate[:, 1:2], ALU.is_equal, ALU.mult)\
                   .then_inc(router_step, 1)
                dve.wait_ge(router_step, count(tile, 9, 8))
                dve.tensor_tensor(w_dense[:, :], gate_a[:, :], gate_b[:, :], ALU.add).then_inc(router_step, 1)
                dve.wait_ge(router_step, count(tile, 9, 9))
                dve.tensor_tensor(h[:, :].rearrange("p (e r) -> p e r", r=R),
                                  lr_ps(tile)[:, 0:ER].rearrange("p (e r) -> p e r", r=R),
                                  w_dense[:, :].unsqueeze(2).to_broadcast([P, E, R]),
                                  ALU.mult).then_inc(h_done, 1)

            def hT_low(tile):
                dve.wait_ge(hT_hi_done, count(tile, 1, 1))
                dve.tensor_tensor(hT_lo[:, :], h_ps[:, 0:P], hT_hi[:, :].bitcast(f32),
                                  ALU.subtract).then_inc(hT_split, 1)

            def add_base(tile, g):
                o0, n = OUTS[g]
                xg = x[:, slot(tile), o0:o0 + n]
                dve.wait_ge(base_done, count(tile, G, g + 1))
                dve.tensor_tensor(xg, base_bank(tile, g)[:, 0:n], xg, ALU.add).then_inc(out_done, 1)

            def step(tile):
                b, j = tile
                nxt, nxt2 = after(tile, 1), after(tile, 2)
                if exists(nxt2):
                    norm1_stats(nxt2)
                if j == TPB - 2 and exists((b, TPB)):
                    mask(b + 1)
                router_top(tile)
                if exists(nxt):
                    norm2(nxt, 0)
                    norm2(nxt, 1)
                if j == TPB - 3 and exists((b, TPB)):
                    ctx_centre(b + 1)
                router_gate(tile)
                if exists(nxt2):
                    softmax_scores(nxt2)
                if exists(nxt):
                    x2_transposes(nxt, range(Q - 1))
                if exists(nxt2):
                    softmax_split(nxt2)
                if exists(nxt):
                    x2_transposes(nxt, range(Q - 1, Q))
                hT_low(tile)
                if j == TPB - 4 and exists((b, TPB)):
                    ctx_sum_chunks(b + 1)
                if j == TPB - 3 and exists((b, TPB)):
                    ctxT_low(b + 1)
                if exists(nxt):
                    x2T_low(nxt)
                if exists(nxt2):
                    add_readout(nxt2)
                    norm2_stats(nxt2)
                for g in range(G):
                    add_base(tile, g)

            dve.sem_inc(out_done, FREE)
            dve.wait_ge(constants_ready, CONSTANTS)
            ctx_sum_chunks(0)
            ctx_centre(0)
            ctxT_low(0)
            for i in range(2):
                xT_low((0, 0), i)
            norm1_stats((0, 0))
            mask(0)
            softmax_scores((0, 0))
            softmax_split((0, 0))
            w_low(dve, 0, 0)
            w_low(dve, 0, 1)
            add_readout((0, 0))
            norm2_stats((0, 0))
            norm1_stats((0, 1))
            softmax_scores((0, 1))
            for g in range(Q):
                norm2((0, 0), g)
            softmax_split((0, 1))
            x2_transposes((0, 0), range(Q))
            x2T_low((0, 0))
            add_readout((0, 1))
            norm2_stats((0, 1))
            for r in range(WPARTS):
                w_low(dve, 1, r)
            with dve.Fori(0, NB - 1) as b:
                for j in range(TPB):
                    step((b, j))
            for j in range(TPB):
                step((NB - 1, j))

        @block.tensor
        def _(pe):
            def three(out_, a_hi, a_lo, w_h, w_l, start, stop, again=False):
                pe.matmul(out_, a_hi, w_h, start=start, stop=False, skip_group_check=again)
                pe.matmul(out_, a_hi, w_l, start=False, stop=False, skip_group_check=again)
                return pe.matmul(out_, a_lo, w_h, start=False, stop=stop, skip_group_check=again)

            def ctx_mean(b):
                pe.wait_ge(ctx_sum_done, b + 1)
                pe.matmul(h_ps[:, P:P + M], one_dth[:, :], ctx_sum[:, :], start=True, stop=True).then_inc(ctx_mean_done, 1)

            def pair_scores(tile):
                b, j = tile
                if j % TPB == 0:
                    pe.wait_ge(ctxT_split, b + j // TPB + 1)
                for c in range(C):
                    if c % HC == 0:
                        pe.wait_ge(xT_split, pairs(tile, 2, c // HC + 1))
                    pe.matmul(s_ps[:, 0:T2], ctxT[:, c, :], xT_hi[:, c, :], start=(c == 0), stop=False)
                    mm = pe.matmul(s_ps[:, 0:T2], ctxT[:, c, :], xT_lo[:, c, :], start=False, stop=(c == C - 1))
                mm.then_inc(sT_done, 1)

            def scores(tile):
                k = tile[1] % 2
                pe.wait_ge(sT_copied, pairs(tile, 1, 1))
                pe.wait_ge(x1_done, count(tile, 2))
                pe.transpose(st_ps, sT[:, k * P:(k + 1) * P], ident[:, :]).then_inc(scores_done, 1)

            def e_transpose(tile):
                pe.wait_ge(e_split_done, count(tile, 1, 1))
                pe.transpose(et_ps, e_split[:, :].bitcast(f32), ident[:, :]).then_inc(eT_done, 1)

            def readout(tile):
                b, j = tile
                if j % TPB == 0:
                    pe.wait_ge(ctx_split, b + j // TPB + 1)
                pe.wait_ge(eT_copied, count(tile, 1, 1))
                for i in range(2):
                    pe.matmul(half(ro_ps, i), eT[:, :], half(ctx_hi, i), start=True, stop=False)
                    pe.matmul(half(ro_ps, i), eT[:, :], half(ctx_lo, i), start=False, stop=True)\
                      .then_inc(readout_done, 1)

            def base(tile, g, chunks_):
                k = tile[1] % 2
                ps_ = base_bank(tile, g)[:, 0:GROUPS[g][1]]
                if chunks_[0] == 0:
                    if tile[1] == 0:
                        pe.wait_ge(w_split[g], WPARTS)
                    pe.wait_ge(out_done, count(tile, G, FREE - len(base_ps[g]) * G + g + 1))
                for c in chunks_:
                    if g == 0 and c % HC == 0:
                        pe.wait_ge(x2T_split, count(tile, 2, c // HC + 1))
                    mm = three(ps_, xT2_hi[:, k, c, :], xT2_lo[:, k, c, :], w_columns(w_hi, g)[:, c, :],
                               w_columns(w_lo, g)[:, c, :], c == 0, g == 0 and c == C - 1)
                if g == 0 and c == C - 1:
                    mm.then_inc(lr_done, 1)

            def h_transpose(tile):
                pe.wait_ge(h_done, count(tile, 1, 1))
                pe.transpose(h_ps[:, 0:P], h[:, :], ident[:, :]).then_inc(hT_done, 1)

            def lora_second(tile, g):
                o0, n = OUTS[g]
                if tile[1] == 0:
                    pe.wait_ge(b_split, 1)
                pe.wait_ge(hT_split, count(tile, 1, 1))
                three(base_bank(tile, g)[:, 0:n], hT_hi[:, :], hT_lo[:, :], b_hi[:, o0:o0 + n], b_lo[:, o0:o0 + n],
                      False, True, again=(g == 0)).then_inc(base_done, 1)

            def step(tile):
                b, j = tile
                nxt, nxt2 = after(tile, 1), after(tile, 2)
                base(tile, 0, range(C))
                if j == TPB - 3 and exists((b, TPB)):
                    ctx_mean(b + 1)
                if j % 2 == 0 and exists(nxt2):
                    pair_scores(nxt2)
                base(tile, 1, range(5))
                if exists(nxt2):
                    scores(nxt2)
                base(tile, 1, range(5, C))
                if j == TPB - 3 and exists((b, TPB)):
                    pe.wait_ge(ctx_centred, b + 2)
                h_transpose(tile)
                c = 2 if j % 2 == 0 else 5
                base(tile, 2, range(c))
                if exists(nxt2):
                    e_transpose(nxt2)
                base(tile, 2, range(c, c + 2))
                if exists(nxt2):
                    readout(nxt2)
                base(tile, 2, range(c + 2, C))
                for g in range(G):
                    lora_second(tile, g)

            pe.wait_ge(constants_ready, CONSTANTS)
            ctx_mean(0)
            pair_scores((0, 0))
            scores((0, 0))
            e_transpose((0, 0))
            readout((0, 0))
            scores((0, 1))
            e_transpose((0, 1))
            readout((0, 1))
            with pe.Fori(0, NB - 1) as b:
                for j in range(TPB):
                    step((b, j))
            for j in range(TPB):
                step((NB - 1, j))


def kernel(x, ctx_2048, mask_BxS2_bk0, L0_ffn_weight, L0_ffn_lora_A, L0_ffn_lora_B, L0_ffn_router_w):
    import numpy as np
    import concourse.bacc as bacc
    from concourse import mybir as mb
    from concourse.bass_utils import run_bass_kernel_spmd

    P = 128

    def by_contraction(a):
        n, d = a.shape
        return np.ascontiguousarray(a.T.reshape(d // P, P, n).transpose(1, 0, 2))

    def by_quadrants(a):
        n, d = a.shape
        return np.ascontiguousarray(a.T.reshape(4, d // P, P // 4, n).transpose(0, 2, 1, 3).reshape(P, d // P, n))

    x, ctx, mask = np.asarray(x), np.asarray(ctx_2048), np.asarray(mask_BxS2_bk0)
    weight, lora_a, lora_b, router = (
        np.asarray(a) for a in (L0_ffn_weight, L0_ffn_lora_A, L0_ffn_lora_B, L0_ffn_router_w))
    B, S, D = x.shape
    E, R, _ = lora_a.shape
    O = weight.shape[0]
    w0 = O - 2 * ((O + E * R + E) // 6 * 2)
    arrays = {
        "x": np.ascontiguousarray(x.reshape(B * S // P, P, D)),
        "xT": np.stack([by_contraction(rows) for rows in x.reshape(B * S // (2 * P), 2 * P, D)]),
        "ctx": np.ascontiguousarray(ctx),
        "ctxT": np.stack([by_contraction(rows) for rows in ctx]),
        "mask": np.ascontiguousarray(mask),
        "wT": by_quadrants(np.concatenate([weight[:w0], lora_a.reshape(E * R, D), router, weight[w0:]])),
        "bT": np.ascontiguousarray(lora_b.transpose(0, 2, 1).reshape(E * R, O)),
    }
    nc = bacc.Bacc("TRN2", target_bir_lowering=False, num_devices=1)
    args = [nc.dram_tensor(f"in_{n}", a.shape, mb.dt.from_np(a.dtype), kind="ExternalInput").ap()
            for n, a in arrays.items()]
    out = nc.dram_tensor("out", (B * S // P, P, O), mb.dt.float32, kind="ExternalOutput").ap()
    xattn_lora_moe_kernel(nc, *args, out)
    r = run_bass_kernel_spmd(nc, [{f"in_{n}": a for n, a in arrays.items()}], core_ids=[0])
    return r.results[0]["out"].reshape(B, S, O)
```
